# Optimizing a Trainium2 kernel written in Bass

```python
import numpy as np
import jax
import jax.numpy as jnp

def _softmax(x, axis=-1):
    return jax.nn.softmax(x, axis=axis)

def _gelu(x):
    return jax.nn.gelu(x, approximate=True)

def _silu(x):
    return jax.nn.silu(x)

def _sigmoid(x):
    return jax.nn.sigmoid(x)

def _layernorm(x, axis=-1, eps=1e-05):
    m = jnp.mean(x, axis=axis, keepdims=True)
    v = jnp.var(x, axis=axis, keepdims=True)
    return (x - m) / jnp.sqrt(v + eps)

def _scatter_add(tgt, idx, src, axis=0):
    return tgt.at[idx].add(src)

def _segment_sum(src, seg, n):
    return jax.ops.segment_sum(src, seg, n)
kernel_name = 'mk_perceiver_d1_seqx_r4_d71b80'

def setup_inputs(seed: int=0):
    np.random.seed(seed)
    _w = jnp.asarray

    def _rec_inputs():
        import jax
        import jax.numpy as jnp
        _rk = jax.random.key(seed)
        x = 7.22e-05 + 1 * jax.random.normal(jax.random.fold_in(_rk, 1), (1, 128, 256), jnp.float32)
        _lenS = 128 - jax.random.randint(jax.random.fold_in(_rk, 7), (1,), 0, max(1, 128 // 4) + 1, jnp.int32)
        _lenS2 = 12544 - jax.random.randint(jax.random.fold_in(_rk, 8), (1,), 0, max(1, 12544 // 4) + 1, jnp.int32)
        _ctx_1024P = jax.random.normal(jax.random.fold_in(_rk, 11), (1, 16, 256), jnp.float32)
        _ctx_1024c = jax.random.dirichlet(jax.random.fold_in(_rk, 511), 0.3 * jnp.ones((16,), jnp.float32), (1, 12544))
        _ctx_1024t = jnp.einsum('bsk,bkd->bsd', _ctx_1024c, _ctx_1024P)
        _ctx_1024t = _ctx_1024t * jax.lax.rsqrt(jnp.mean(jnp.square(_ctx_1024t)) + 1e-12) * 0.953939
        ctx_1024 = -0.000514642 + 1.00011 * (_ctx_1024t + 0.3 * jax.random.normal(jax.random.fold_in(_rk, 611), (1, 12544, 256), jnp.float32))
        return (x, ctx_1024)
    x, ctx_1024 = _rec_inputs()

    def _L0_xattn_setup():
        import jax, jax.numpy as jnp
        import numpy as np
        B, L_ENC, L_DEC, D = (16, 128, 128, 256)
        key = jax.random.key(seed)
        k1, k2, k3, k4, k5, k6 = jax.random.split(key, 6)
        encoder_hc = jax.random.normal(k1, (B, L_ENC, D), dtype=jnp.float32)
        decoder_hq = jax.random.normal(k2, (B, L_DEC, D), dtype=jnp.float32)
        w_sim = jax.random.normal(k3, (3 * D,), dtype=jnp.float32) * 0.02
        b_sim = jax.random.normal(k4, (1,), dtype=jnp.float32) * 0.02
        W_qv = jax.random.normal(k5, (4 * D, D), dtype=jnp.float32) * 0.02
        b_qv = jax.random.normal(k6, (D,), dtype=jnp.float32) * 0.02
        return {'encoder_hc': encoder_hc, 'decoder_hq': decoder_hq, 'w_sim': w_sim, 'b_sim': b_sim, 'W_qv': W_qv, 'b_qv': b_qv}
    _L0_xattn_all = _L0_xattn_setup()
    _L0_xattn_in = {k: v for k, v in _L0_xattn_all.items() if k in ('w_sim', 'b_sim', 'W_qv', 'b_qv')}
    del _L0_xattn_all

    def _L0_attn_setup():
        import math
        import jax, jax.numpy as jnp
        import numpy as np
        N_HEAD = 16

        def _rope_cos_sin(l, head_dim):
            scale = jnp.arange(0, head_dim, 2, dtype=jnp.float32)[:head_dim // 2]
            freqs = 1.0 / 10000.0 ** scale
            angles = jnp.arange(l, dtype=jnp.float32)[:, None] * freqs[None, :]
            return (jnp.cos(angles), jnp.sin(angles))

        def _rope_apply(x, cos, sin):
            b, l, h, hd = x.shape
            xp = x.astype(jnp.float32).reshape(b, l, h, hd // 2, 2)
            xr, xi = (xp[..., 0], xp[..., 1])
            c = cos[None, :, None, :]
            s = sin[None, :, None, :]
            out_r = xr * c - xi * s
            out_i = xr * s + xi * c
            out = jnp.stack([out_r, out_i], axis=-1).reshape(b, l, h, hd)
            return out.astype(x.dtype)
        key = jax.random.key(seed)
        ks = jax.random.split(key, 9)
        b, l, d = (2, 512, 256)
        sc = 1.0 / math.sqrt(d)
        inp = {'x': jax.random.normal(ks[0], (b, l, d), dtype=jnp.float32), 'Wq': jax.random.normal(ks[1], (d, d), dtype=jnp.float32) * sc, 'bq': jnp.zeros((d,), dtype=jnp.float32), 'Wk': jax.random.normal(ks[2], (d, d), dtype=jnp.float32) * sc, 'bk': jnp.zeros((d,), dtype=jnp.float32), 'Wv': jax.random.normal(ks[3], (d, d), dtype=jnp.float32) * sc, 'bv': jnp.zeros((d,), dtype=jnp.float32), 'Wo': jax.random.normal(ks[4], (d, d), dtype=jnp.float32) * sc, 'bo': jnp.zeros((d,), dtype=jnp.float32)}
        return inp
    _L0_attn_all = _L0_attn_setup()
    _L0_attn_in = {k: v for k, v in _L0_attn_all.items() if k in ('Wq', 'bq', 'Wk', 'bk', 'Wv', 'bv', 'Wo', 'bo')}
    del _L0_attn_all

    def _L0_ffn_setup():
        import jax, jax.numpy as jnp
        import numpy as np
        DIM = 256

        def _reference_tuple_inner(x, W_r, W_k, W_v, mu_r, mu_k):
            B, T, C = x.shape
            x_prev = jnp.concatenate([jnp.zeros((B, 1, C), x.dtype), x[:, :-1, :]], axis=1)
            xr = mu_r * x + (1.0 - mu_r) * x_prev
            xk = mu_k * x + (1.0 - mu_k) * x_prev
            r = jax.nn.sigmoid(jnp.einsum('btc,dc->btd', xr, W_r))
            k = jnp.einsum('btc,dc->btd', xk, W_k)
            k_act = jnp.square(jax.nn.relu(k))
            out = r * jnp.einsum('btc,dc->btd', k_act, W_v)
            new_state = x[:, -1, :]
            return (out, new_state)
        key = jax.random.key(seed)
        ks = jax.random.split(key, 6)
        B, T, C = (8, 512, DIM)
        x = jax.random.normal(ks[0], (B, T, C), dtype=jnp.float32)
        s = 1.0 / np.sqrt(C)
        W_r = jax.random.uniform(ks[1], (C, C), jnp.float32, -s, s)
        W_k = jax.random.uniform(ks[2], (C, C), jnp.float32, -s, s)
        W_v = jax.random.uniform(ks[3], (C, C), jnp.float32, -s, s)
        mu_r = jax.random.uniform(ks[4], (C,), jnp.float32)
        mu_k = jax.random.uniform(ks[5], (C,), jnp.float32)
        return {'x': x, 'W_r': W_r, 'W_k': W_k, 'W_v': W_v, 'mu_r': mu_r, 'mu_k': mu_k}
    _L0_ffn_all = _L0_ffn_setup()
    _L0_ffn_in = {k: v for k, v in _L0_ffn_all.items() if k in ('W_r', 'W_k', 'W_v', 'mu_r', 'mu_k')}
    del _L0_ffn_all
    return {'x': x, 'ctx_1024': ctx_1024, 'L0_xattn_w_sim': _L0_xattn_in['w_sim'], 'L0_xattn_b_sim': _L0_xattn_in['b_sim'], 'L0_xattn_W_qv': _L0_xattn_in['W_qv'], 'L0_xattn_b_qv': _L0_xattn_in['b_qv'], 'L0_attn_Wq': _L0_attn_in['Wq'], 'L0_attn_bq': _L0_attn_in['bq'], 'L0_attn_Wk': _L0_attn_in['Wk'], 'L0_attn_bk': _L0_attn_in['bk'], 'L0_attn_Wv': _L0_attn_in['Wv'], 'L0_attn_bv': _L0_attn_in['bv'], 'L0_attn_Wo': _L0_attn_in['Wo'], 'L0_attn_bo': _L0_attn_in['bo'], 'L0_ffn_W_r': _L0_ffn_in['W_r'], 'L0_ffn_W_k': _L0_ffn_in['W_k'], 'L0_ffn_W_v': _L0_ffn_in['W_v'], 'L0_ffn_mu_r': _L0_ffn_in['mu_r'], 'L0_ffn_mu_k': _L0_ffn_in['mu_k']}

def reference(x, ctx_1024, L0_xattn_w_sim, L0_xattn_b_sim, L0_xattn_W_qv, L0_xattn_b_qv, L0_attn_Wq, L0_attn_bq, L0_attn_Wk, L0_attn_bk, L0_attn_Wv, L0_attn_bv, L0_attn_Wo, L0_attn_bo, L0_ffn_W_r, L0_ffn_W_k, L0_ffn_W_v, L0_ffn_mu_r, L0_ffn_mu_k):
    import jax
    import jax.numpy as jnp

    def _L0_xattn_ref(encoder_hc, decoder_hq, w_sim, b_sim, W_qv, b_qv):
        import jax, jax.numpy as jnp
        import numpy as np
        B, L_ENC, L_DEC, D = (16, 128, 128, 256)
        d = encoder_hc.shape[-1]
        w1, w2, w3 = (w_sim[:d], w_sim[d:2 * d], w_sim[2 * d:])
        Sim = (encoder_hc @ w1)[:, :, None] + (decoder_hq @ w2)[:, None, :] + jnp.einsum('bid,bjd->bij', encoder_hc * w3, decoder_hq) + b_sim[0]
        A = jax.nn.softmax(Sim, axis=2)
        hq_hat = jnp.einsum('bij,bjd->bid', A, decoder_hq)
        Batt = jax.nn.softmax(jnp.max(Sim, axis=2), axis=1)
        hc_bar = jnp.einsum('bi,bid->bd', Batt, encoder_hc)[:, None, :]
        hc_hat = jnp.broadcast_to(hc_bar, encoder_hc.shape)
        feats = jnp.concatenate([encoder_hc, hq_hat, encoder_hc * hq_hat, encoder_hc * hc_hat], axis=-1)
        hcq = feats @ W_qv + b_qv
        return hcq

    def _L0_attn_ref(x, Wq, bq, Wk, bk, Wv, bv, Wo, bo):
        import math
        import jax, jax.numpy as jnp
        import numpy as np
        N_HEAD = 16

        def _rope_cos_sin(l, head_dim):
            scale = jnp.arange(0, head_dim, 2, dtype=jnp.float32)[:head_dim // 2]
            freqs = 1.0 / 10000.0 ** scale
            angles = jnp.arange(l, dtype=jnp.float32)[:, None] * freqs[None, :]
            return (jnp.cos(angles), jnp.sin(angles))

        def _rope_apply(x, cos, sin):
            b, l, h, hd = x.shape
            xp = x.astype(jnp.float32).reshape(b, l, h, hd // 2, 2)
            xr, xi = (xp[..., 0], xp[..., 1])
            c = cos[None, :, None, :]
            s = sin[None, :, None, :]
            out_r = xr * c - xi * s
            out_i = xr * s + xi * c
            out = jnp.stack([out_r, out_i], axis=-1).reshape(b, l, h, hd)
            return out.astype(x.dtype)
        b, l, d = x.shape
        h = N_HEAD
        hd = d // h
        q = (x @ Wq + bq).reshape(b, l, h, hd)
        k = (x @ Wk + bk).reshape(b, l, h, hd)
        v = (x @ Wv + bv).reshape(b, l, h, hd)
        cos, sin = _rope_cos_sin(l, hd)
        q = _rope_apply(q, cos, sin)
        k = _rope_apply(k, cos, sin)
        score = jnp.einsum('blhd,bmhd->bhlm', q, k) / math.sqrt(hd)
        ctx = jnp.einsum('bhlm,bmhd->blhd', score, v).reshape(b, l, d)
        return ctx @ Wo + bo

    def _L0_ffn_ref(x, W_r, W_k, W_v, mu_r, mu_k):
        import jax, jax.numpy as jnp
        import numpy as np
        DIM = 256

        def _reference_tuple_inner(x, W_r, W_k, W_v, mu_r, mu_k):
            B, T, C = x.shape
            x_prev = jnp.concatenate([jnp.zeros((B, 1, C), x.dtype), x[:, :-1, :]], axis=1)
            xr = mu_r * x + (1.0 - mu_r) * x_prev
            xk = mu_k * x + (1.0 - mu_k) * x_prev
            r = jax.nn.sigmoid(jnp.einsum('btc,dc->btd', xr, W_r))
            k = jnp.einsum('btc,dc->btd', xk, W_k)
            k_act = jnp.square(jax.nn.relu(k))
            out = r * jnp.einsum('btc,dc->btd', k_act, W_v)
            new_state = x[:, -1, :]
            return (out, new_state)
        return _reference_tuple_inner(x, W_r, W_k, W_v, mu_r, mu_k)[0]
    x = x + _L0_xattn_ref(_layernorm(x, axis=-1), ctx_1024, L0_xattn_w_sim, L0_xattn_b_sim, L0_xattn_W_qv, L0_xattn_b_qv)
    x = x + _L0_attn_ref(_layernorm(x, axis=-1), L0_attn_Wq, L0_attn_bq, L0_attn_Wk, L0_attn_bk, L0_attn_Wv, L0_attn_bv, L0_attn_Wo, L0_attn_bo)
    x = x + _L0_ffn_ref(_layernorm(x, axis=-1), L0_ffn_W_r, L0_ffn_W_k, L0_ffn_W_v, L0_ffn_mu_r, L0_ffn_mu_k)
    return x

_drawn_inputs = setup_inputs


def setup_inputs(seed=0):
    import zlib

    import numpy as np

    out = dict(_drawn_inputs(seed))
    spreads = {'L0_attn_bq': (0.0, 0.1),
     'L0_attn_bk': (0.0, 0.1),
     'L0_attn_bv': (0.0, 0.1),
     'L0_attn_bo': (0.0, 2.0)}
    factors = {'L0_ffn_W_r': 8.0,
     'L0_ffn_W_k': 8.0,
     'L0_ffn_W_v': 8.0,
     'L0_ffn_mu_r': 8.0,
     'L0_ffn_mu_k': 8.0}
    for name, (base, spread) in spreads.items():
        noise = np.random.default_rng([zlib.crc32(name.encode()), seed]).standard_normal(out[name].shape)
        drawn = base * np.exp(spread * noise) if base else spread * noise
        out[name] = jnp.asarray(drawn.astype(out[name].dtype))
    for name, factor in factors.items():
        out[name] = (out[name] * factor).astype(out[name].dtype)
    return out
```

```python
from contextlib import ExitStack

import numpy as np

import concourse.bass as bass
from concourse import mybir

P = 128
F32 = mybir.dt.float32
F32R = mybir.dt.float32r
BF16 = mybir.dt.bfloat16
ALU = mybir.AluOpType
ACT = mybir.ActivationFunctionType
AX_X = mybir.AxisListType.X

L = 128
D = 256
DH = D // P
HEADS = 16
HEAD_D = D // HEADS
S = 12544
TILES = 4
CHUNK = TILES * P
RING = 4
FULL = S // CHUNK
LAST_TILES = (S - FULL * CHUNK) // P
CHUNKS = FULL + 1
LOOPED = (FULL - RING) // RING * RING
EPS = 1e-5
GATE_FLOOR = -87.0
FAR_BELOW = 3.0e38

WB_QV = 0
WB_QK = 4 * DH
WB_V = WB_QK + 2 * DH
WB_O = WB_V + DH
WB_FK = WB_O + DH
WB_FR = WB_FK + DH
WB_FV = WB_FR + DH
WB = WB_FV + DH

VC_W1, VC_W2, VC_W3, VC_MUR, VC_MUK = (DH * n for n in range(5))
BR_QV, BR_O, BR_Q, BR_V, BR_SIM = 0, D, 2 * D, 4 * D, 5 * D
BR = 5 * D + 1
C_ID, C_MASK, C_ONES, C_COS = 0, P, 2 * P, 3 * P
C_SIN = C_COS + 2 * D
C_ALL = C_SIN + 2 * D


def build(nc, x, ctx_in, weights_in, vec_in, bias_in, const_in, out):
    ctx_full = ctx_in[0:FULL * CHUNK, :].rearrange("(k p t) d -> k p (t d)", p=P, t=TILES)
    ctx_last = ctx_in[FULL * CHUNK:S, :].rearrange("(p t) d -> p (t d)", t=LAST_TILES)

    with ExitStack() as stack:
        def sb(name, shape, dt=F32):
            return stack.enter_context(nc.sbuf_tensor(name, shape, dt))

        def ps(name, shape, dt=F32):
            return stack.enter_context(nc.psum_tensor(name, shape, dt))

        def sem(name):
            return stack.enter_context(nc.semaphore(name))

        const = sb("const", [P, C_ALL])
        ident = const[:, C_ID:C_ID + P]
        block_mask = const[:, C_MASK:C_MASK + P]
        ones = const[:, C_ONES:C_ONES + P]
        rope_cos = const[:, C_COS:C_COS + 2 * D]
        rope_sin = const[:, C_SIN:C_SIN + 2 * D]
        w = sb("w", [P, WB, D])
        vec = sb("vec", [P, 5 * DH])
        bias = sb("bias", [1, BR])
        x_sb = sb("x_sb", [P, D])
        ctx_rows = sb("ctx_rows", [P, RING, TILES, D])

        ctx_high = sb("ctx_high", [P, 2, DH, CHUNK], F32R)
        ctx_low = sb("ctx_low", [P, 2, DH, CHUNK], F32R)
        probs = sb("probs", [P, 2, CHUNK])
        probs_turned = sb("probs_turned", [P, 2, TILES, P])
        unused = sb("unused", [P, CHUNK], BF16)
        neg_max = sb("neg_max", [P, RING])
        rescale = sb("rescale", [P, RING])
        row_sum = sb("row_sum", [P, RING])
        acc = sb("acc", [P, D])
        total = sb("total", [P, 1])

        ln_six = sb("ln_six", [P, 3, 6])
        ln_mv = sb("ln_mv", [P, 3, 2])
        ln_var = sb("ln_var", [P, 3])
        ln_rstd = sb("ln_rstd", [P, 3])
        minus_half = sb("minus_half", [P, 1])
        normed = sb("normed", [P, 3, D])
        normed_t = sb("normed_t", [P, 2, DH, P])
        q_t = sb("q_t", [P, DH, P])
        q_high = sb("q_high", [P, DH, P], F32R)
        q_low = sb("q_low", [P, DH, P], F32R)
        warm = sb("warm", [P, 1])

        sim_max = sb("sim_max", [P, 1])
        batt_neg_max = sb("batt_neg_max", [P, 1])
        batt = sb("batt", [P, 1])
        batt_inv = sb("batt_inv", [P, 1])
        hc_hat_t = sb("hc_hat_t", [P, DH, P])
        total_inv = sb("total_inv", [P, 1])
        hq = sb("hq", [P, D])
        hq_t = sb("hq_t", [P, DH, P])
        h_hq_t = sb("h_hq_t", [P, DH, P])
        x1 = sb("x1", [P, D])

        qk_cos = sb("qk_cos", [P, 2 * D])
        qk_sin = sb("qk_sin", [P, 2 * D])
        qk = sb("qk", [P, 2 * D])
        v = sb("v", [P, D])
        q_rot_t = sb("q_rot_t", [P, DH, P])
        kv = sb("kv", [P, DH, P])
        heads_t = sb("heads_t", [P, DH, P])
        x2 = sb("x2", [P, D])

        shifted = sb("shifted", [P, DH, P + 1])
        step_t = sb("step_t", [P, DH, P])
        xk_t = sb("xk_t", [P, DH, P])
        xr_t = sb("xr_t", [P, DH, P])
        k_relu = sb("k_relu", [P, DH, P])
        k_act = sb("k_act", [P, DH, P])
        gate_in = sb("gate_in", [P, D])
        gate_exp = sb("gate_exp", [P, D])
        gate_den = sb("gate_den", [P, D])
        gate = sb("gate", [P, D])
        mixed_out = sb("mixed_out", [P, D])
        x3 = sb("x3", [P, D])

        ctx_turned_ps = ps("ctx_turned_ps", [P, DH, CHUNK])
        scores_ps = ps("scores_ps", [P, 2, CHUNK])
        probs_turned_ps = ps("probs_turned_ps", [P, 2, CHUNK])
        mixed_ps = ps("mixed_ps", [P, CHUNK])
        side_ps = ps("side_ps", [P, CHUNK])
        hcq_ps = side_ps[:, 0:D]

        x_loaded = sem("x_loaded")
        const_loaded = sem("const_loaded")
        vec_loaded = sem("vec_loaded")
        bias_loaded = sem("bias_loaded")
        w_loaded = sem("w_loaded")
        ctx_loaded = [sem(f"ctx_loaded{r}") for r in range(RING)]
        out_stored = sem("out_stored")

        minus_half_set = sem("minus_half_set")
        shift_zeroed = sem("shift_zeroed")
        stats_done = sem("stats_done")
        mv_done = sem("mv_done")
        var_done = sem("var_done")
        rstd_done = sem("rstd_done")
        normed_done = sem("normed_done")
        normed_turned = sem("normed_turned")
        normed_t_done = sem("normed_t_done")
        q_done = sem("q_done")
        q_high_done = sem("q_high_done")
        q_low_done = sem("q_low_done")

        ctx_turned = sem("ctx_turned")
        high_done = sem("high_done")
        low_done = sem("low_done")
        scores_done = sem("scores_done")
        max_done = sem("max_done")
        exp_done = sem("exp_done")
        rescale_done = sem("rescale_done")
        probs_turned_done = sem("probs_turned_done")
        probs_copied = sem("probs_copied")
        mixed_done = sem("mixed_done")
        acc_done = sem("acc_done")
        total_done = sem("total_done")

        hw1_done = sem("hw1_done")
        sim_max_done = sem("sim_max_done")
        sim_max_spread = sem("sim_max_spread")
        batt_max_done = sem("batt_max_done")
        batt_done = sem("batt_done")
        hc_bar_done = sem("hc_bar_done")
        batt_inv_done = sem("batt_inv_done")
        hc_hat_done = sem("hc_hat_done")
        total_inv_done = sem("total_inv_done")
        hq_done = sem("hq_done")
        hq_turned = sem("hq_turned")
        hq_t_done = sem("hq_t_done")
        h_hq_done = sem("h_hq_done")
        hcq_done = sem("hcq_done")
        x1_done = sem("x1_done")

        qk_projected = sem("qk_projected")
        v_projected = sem("v_projected")
        cos_done = sem("cos_done")
        sin_done = sem("sin_done")
        qk_done = sem("qk_done")
        v_done = sem("v_done")
        q_rot_turned = sem("q_rot_turned")
        q_rot_t_done = sem("q_rot_t_done")
        kv_done = sem("kv_done")
        kv_masked = sem("kv_masked")
        heads_done = sem("heads_done")
        heads_copied = sem("heads_copied")
        attn_done = sem("attn_done")
        x2_done = sem("x2_done")

        step_done = sem("step_done")
        xk_done = sem("xk_done")
        xr_done = sem("xr_done")
        k_projected = sem("k_projected")
        r_projected = sem("r_projected")
        k_relu_done = sem("k_relu_done")
        k_act_done = sem("k_act_done")
        gate_in_done = sem("gate_in_done")
        gate_exp_done = sem("gate_exp_done")
        gate_den_done = sem("gate_den_done")
        gate_done = sem("gate_done")
        mix_done = sem("mix_done")
        mixed_out_done = sem("mixed_out_done")
        x3_done = sem("x3_done")

        block = stack.enter_context(nc.Block())

        def tiles_of(k):
            return LAST_TILES if isinstance(k, int) and k == CHUNKS - 1 else TILES

        @block.sync
        def _(sp):
            sp.dma_start(x_sb[:, :], x).then_inc(x_loaded, 16)
            for k in range(RING):
                sp.dma_start(ctx_rows[:, k, :, :], ctx_full[k].rearrange("p (t d) -> p t d", t=TILES))\
                    .then_inc(ctx_loaded[k], 16)
            sp.dma_start(w[:, :, :], weights_in.rearrange("p (b n) -> p b n", b=WB)).then_inc(w_loaded, 16)
            with sp.Fori(0, (FULL - RING) // RING) as turn_of_ring:
                base = turn_of_ring * RING
                for u in range(RING):
                    sp.wait_ge(mixed_done, base + (u + 1))
                    src = ctx_full[bass.ds(base + (u + RING), 1), :, :]
                    sp.dma_start(ctx_rows[:, u, :, :], src.rearrange("k p (t d) -> p (k t) d", t=TILES))\
                        .then_inc(ctx_loaded[u], 16)
            k = CHUNKS - 1
            sp.wait_ge(mixed_done, k - RING + 1)
            sp.dma_start(ctx_rows[:, k % RING, 0:LAST_TILES, :],
                         ctx_last.rearrange("p (t d) -> p t d", t=LAST_TILES)).then_inc(ctx_loaded[k % RING], 16)
            sp.wait_ge(x3_done, 1)
            sp.dma_start(out, x3[:, :]).then_inc(out_stored, 16)
            sp.wait_ge(out_stored, 16)

        @block.gpsimd
        def _(pool):
            nc.gpsimd.memset(minus_half[:, :], -0.5).then_inc(minus_half_set, 1)
            nc.gpsimd.memset(shifted[:, :, 0:1], 0.0).then_inc(shift_zeroed, 1)
            pool.wait_ge(minus_half_set, 1)
            for n in range(3):
                pool.wait_ge(var_done, n + 1)
                nc.gpsimd.tensor_tensor(out=ln_rstd[:, n:n + 1], in0=ln_var[:, n:n + 1], in1=minus_half[:, :],
                                        op=ALU.pow).then_inc(rstd_done, 1)

        @block.scalar
        def _(act):
            act.dma_start(const[:, :], const_in).then_inc(const_loaded, 16)
            act.dma_start(vec[:, :], vec_in).then_inc(vec_loaded, 16)
            act.dma_start(bias[:, :], bias_in).then_inc(bias_loaded, 16)
            act.wait_ge(minus_half_set, 1)
            nc.scalar.activation(warm[:, :], minus_half[:, :], ACT.Exp)

            def take_high(k, u):
                width = tiles_of(k) * P
                act.wait_ge(ctx_turned, k + 1)
                for a in range(DH):
                    nc.scalar.activation(ctx_high[:, u % 2, a, 0:width], ctx_turned_ps[:, a, 0:width],
                                         ACT.Copy).then_inc(high_done, 1)

            def exps(k, u):
                width = tiles_of(k) * P
                act.wait_ge(max_done, k + 2)
                nc.scalar.activation(probs[:, u % 2, 0:width], scores_ps[:, u % 2, 0:width], ACT.Exp,
                                     bias=neg_max[:, u:u + 1], accum_out=row_sum[:, u:u + 1])\
                    .then_inc(exp_done, 1)
                before = (u - 1) % RING
                nc.scalar.activation(rescale[:, u:u + 1], neg_max[:, before:before + 1], ACT.Exp,
                                     bias=neg_max[:, u:u + 1], scale=-1.0).then_inc(rescale_done, 1)

            take_high(0, 0)
            act.wait_ge(q_done, 1)
            nc.scalar.activation(q_high[:, :, :], q_t[:, :, :], ACT.Copy).then_inc(q_high_done, 1)
            take_high(1, 1)
            exps(0, 0)
            with act.Fori(0, LOOPED // RING) as turn_of_ring:
                base = turn_of_ring * RING
                for u in range(RING):
                    take_high(base + (u + 2), (u + 2) % RING)
                    exps(base + (u + 1), (u + 1) % RING)
            for k in range(LOOPED, CHUNKS):
                if k + 2 < CHUNKS:
                    take_high(k + 2, (k + 2) % RING)
                if k + 1 < CHUNKS:
                    exps(k + 1, (k + 1) % RING)

            act.wait_ge(batt_max_done, 1)
            nc.scalar.activation(batt[:, :], sim_max[:, :], ACT.Exp, bias=batt_neg_max[:, :]).then_inc(batt_done, 1)
            act.wait_ge(hq_turned, 1)
            nc.scalar.activation(hq_t[:, :, :], probs_turned_ps[:, 0, 0:D].rearrange("p (a l) -> p a l", a=DH),
                                 ACT.Copy).then_inc(hq_t_done, 1)
            act.wait_ge(normed_turned, 2)
            nc.scalar.activation(normed_t[:, 1, :, :], probs_turned_ps[:, 0, 0:D].rearrange("p (a l) -> p a l", a=DH),
                                 ACT.Copy).then_inc(normed_t_done, 1)
            act.wait_ge(v_projected, 1)
            nc.scalar.activation(v[:, :], mixed_ps[:, 0:D], ACT.Copy).then_inc(v_done, 1)
            act.wait_ge(q_rot_turned, 1)
            nc.scalar.activation(q_rot_t[:, :, :], probs_turned_ps[:, 0, 0:D].rearrange("p (a l) -> p a l", a=DH),
                                 ACT.Copy).then_inc(q_rot_t_done, 1)
            act.wait_ge(heads_done, 1)
            nc.scalar.activation(heads_t[:, :, :], mixed_ps[:, 0:D].rearrange("p (a l) -> p a l", a=DH),
                                 ACT.Copy).then_inc(heads_copied, 1)
            act.wait_ge(shift_zeroed, 1)
            act.wait_ge(normed_turned, 3)
            nc.scalar.activation(shifted[:, :, 1:P + 1], probs_turned_ps[:, 0, 0:D].rearrange("p (a l) -> p a l", a=DH),
                                 ACT.Copy).then_inc(normed_t_done, 1)
            act.wait_ge(k_relu_done, 1)
            nc.scalar.activation(k_act[:, :, :], k_relu[:, :, :], ACT.Square).then_inc(k_act_done, 1)
            act.wait_ge(gate_in_done, 1)
            nc.scalar.activation(gate_exp[:, :], gate_in[:, :], ACT.Exp, scale=-1.0).then_inc(gate_exp_done, 1)

        @block.vector
        def _(dve):
            def layer_norm(n, source):
                nc.vector.bn_stats(ln_six[:, n, :], source).then_inc(stats_done, 1)
                dve.wait_ge(stats_done, n + 1)
                nc.vector.bn_aggr(ln_mv[:, n, :], ln_six[:, n, :]).then_inc(mv_done, 1)
                dve.wait_ge(mv_done, n + 1)
                nc.vector.tensor_scalar_add(ln_var[:, n:n + 1], ln_mv[:, n, 1:2], EPS).then_inc(var_done, 1)
                dve.wait_ge(rstd_done, n + 1)
                nc.vector.tensor_scalar(normed[:, n, :], source, ln_mv[:, n, 0:1], ln_rstd[:, n:n + 1],
                                        ALU.subtract, ALU.mult).then_inc(normed_done, 1)

            def take_low(k, u):
                width = tiles_of(k) * P
                for a in range(DH):
                    dve.wait_ge(high_done, k * DH + (a + 1))
                    nc.vector.tensor_tensor(out=ctx_low[:, u % 2, a, 0:width], in0=ctx_turned_ps[:, a, 0:width],
                                            in1=ctx_high[:, u % 2, a, 0:width].bitcast(F32), op=ALU.subtract)\
                        .then_inc(low_done, 1)

            def running_max(k, u):
                width = tiles_of(k) * P
                before = (u - 1) % RING
                dve.wait_ge(scores_done, k + 1)
                dve.wait_ge(max_done, k + 1)
                nc.vector.tensor_scalar(unused[:, 0:width], scores_ps[:, u % 2, 0:width], -1.0,
                                        neg_max[:, before:before + 1], ALU.mult, ALU.min,
                                        accum_out=neg_max[:, u:u + 1]).then_inc(max_done, 1)

            def copy_probs(k, u):
                for half in range(tiles_of(k) // 2):
                    dve.wait_ge(probs_turned_done, 2 * k + (half + 1))
                    nc.vector.tensor_copy(probs_turned[:, u % 2, 2 * half:2 * half + 2, :],
                                          probs_turned_ps[:, half, 0:2 * P].rearrange("p (t l) -> p t l", t=2))\
                        .then_inc(probs_copied, 1)

            def accumulate(k, u):
                dve.wait_ge(rescale_done, k + 1)
                dve.wait_ge(exp_done, k + 1)
                dve.wait_ge(total_done, k + 1)
                nc.vector.scalar_tensor_tensor(total[:, :], total[:, :], rescale[:, u:u + 1], row_sum[:, u:u + 1],
                                               ALU.mult, ALU.add).then_inc(total_done, 1)
                dve.wait_ge(mixed_done, k + 1)
                dve.wait_ge(acc_done, k + 1)
                nc.vector.scalar_tensor_tensor(acc[:, :], acc[:, :], rescale[:, u:u + 1], mixed_ps[:, 0:D],
                                               ALU.mult, ALU.add).then_inc(acc_done, 1)

            nc.vector.memset(neg_max[:, RING - 1:RING], FAR_BELOW).then_inc(max_done, 1)
            nc.vector.memset(acc[:, :], 0.0).then_inc(acc_done, 1)
            nc.vector.memset(total[:, :], 0.0).then_inc(total_done, 1)
            dve.wait_ge(x_loaded, 16)
            layer_norm(0, x_sb[:, :])
            dve.wait_ge(normed_turned, 1)
            nc.vector.tensor_copy(normed_t[:, 0, :, :], side_ps[:, 0:D].rearrange("p (a l) -> p a l", a=DH))\
                .then_inc(normed_t_done, 1)
            dve.wait_ge(vec_loaded, 16)
            dve.wait_ge(normed_t_done, 1)
            for a in range(DH):
                last = nc.vector.tensor_scalar(q_t[:, a, :], normed_t[:, 0, a, :], vec[:, VC_W3 + a:VC_W3 + a + 1],
                                               vec[:, VC_W2 + a:VC_W2 + a + 1], ALU.mult, ALU.add)
            last.then_inc(q_done, 1)
            dve.wait_ge(q_high_done, 1)
            nc.vector.tensor_tensor(out=q_low[:, :, :], in0=q_t[:, :, :], in1=q_high[:, :, :].bitcast(F32),
                                    op=ALU.subtract).then_inc(q_low_done, 1)
            take_low(0, 0)
            take_low(1, 1)
            running_max(0, 0)
            with dve.Fori(0, LOOPED // RING) as turn_of_ring:
                base = turn_of_ring * RING
                for u in range(RING):
                    copy_probs(base + u, u)
                    running_max(base + (u + 1), (u + 1) % RING)
                    take_low(base + (u + 2), (u + 2) % RING)
                    accumulate(base + u, u)
            for k in range(LOOPED, CHUNKS):
                copy_probs(k, k % RING)
                if k + 1 < CHUNKS:
                    running_max(k + 1, (k + 1) % RING)
                if k + 2 < CHUNKS:
                    take_low(k + 2, (k + 2) % RING)
                if k == CHUNKS - 2:
                    u = (CHUNKS - 1) % RING
                    dve.wait_ge(hw1_done, 1)
                    dve.wait_ge(max_done, CHUNKS + 1)
                    nc.vector.tensor_tensor(out=sim_max[:, :], in0=side_ps[:, D:D + 1], in1=neg_max[:, u:u + 1],
                                            op=ALU.subtract).then_inc(sim_max_done, 1)
                if k == CHUNKS - 1:
                    dve.wait_ge(sim_max_spread, 1)
                    nc.vector.tensor_reduce(batt_neg_max[:, :], scores_ps[:, 1, 0:P], axis=AX_X, op=ALU.max,
                                            negate=True).then_inc(batt_max_done, 1)
                accumulate(k, k % RING)

            dve.wait_ge(total_done, CHUNKS + 1)
            nc.vector.reciprocal(total_inv[:, :], total[:, :]).then_inc(total_inv_done, 1)
            dve.wait_ge(total_inv_done, 1)
            dve.wait_ge(acc_done, CHUNKS + 1)
            nc.vector.tensor_scalar(hq[:, :], acc[:, :], total_inv[:, :], None, ALU.mult).then_inc(hq_done, 1)
            dve.wait_ge(hc_bar_done, 1)
            nc.vector.reciprocal(batt_inv[:, :], scores_ps[:, 0, DH:DH + 1]).then_inc(batt_inv_done, 1)
            dve.wait_ge(batt_inv_done, 1)
            for a in range(DH):
                last = nc.vector.tensor_scalar(hc_hat_t[:, a, :], normed_t[:, 0, a, :], scores_ps[:, 0, a:a + 1],
                                               batt_inv[:, :], ALU.mult, ALU.mult)
            last.then_inc(hc_hat_done, 1)
            dve.wait_ge(hq_t_done, 1)
            nc.vector.tensor_tensor(out=h_hq_t[:, :, :], in0=normed_t[:, 0, :, :], in1=hq_t[:, :, :],
                                    op=ALU.mult).then_inc(h_hq_done, 1)
            dve.wait_ge(hcq_done, 1)
            nc.vector.tensor_tensor(out=x1[:, :], in0=hcq_ps, in1=x_sb[:, :], op=ALU.add).then_inc(x1_done, 1)

            dve.wait_ge(x1_done, 1)
            layer_norm(1, x1[:, :])
            dve.wait_ge(qk_projected, 1)
            nc.vector.tensor_tensor(out=qk_cos[:, :], in0=scores_ps[:, 0, :], in1=rope_cos, op=ALU.mult)\
                .then_inc(cos_done, 1)
            for part in range(2):
                last = nc.vector.tensor_tensor(out=qk_sin[:, part:2 * D:2], in0=scores_ps[:, 0, 1 - part:2 * D:2],
                                               in1=rope_sin[:, part:2 * D:2], op=ALU.mult)
            last.then_inc(sin_done, 1)
            dve.wait_ge(cos_done, 1)
            dve.wait_ge(sin_done, 1)
            nc.vector.tensor_tensor(out=qk[:, :], in0=qk_cos[:, :], in1=qk_sin[:, :], op=ALU.add).then_inc(qk_done, 1)
            dve.wait_ge(kv_done, 1)
            nc.vector.tensor_tensor(out=kv[:, :, :], in0=ctx_turned_ps[:, :, 0:P],
                                    in1=block_mask.unsqueeze(1).to_broadcast([P, DH, P]), op=ALU.mult)\
                .then_inc(kv_masked, 1)
            dve.wait_ge(attn_done, 1)
            nc.vector.tensor_tensor(out=x2[:, :], in0=side_ps[:, D:2 * D], in1=x1[:, :], op=ALU.add).then_inc(x2_done, 1)

            dve.wait_ge(x2_done, 1)
            layer_norm(2, x2[:, :])
            dve.wait_ge(normed_t_done, 3)
            nc.vector.tensor_tensor(out=step_t[:, :, :], in0=shifted[:, :, 1:P + 1], in1=shifted[:, :, 0:P],
                                    op=ALU.subtract).then_inc(step_done, 1)
            dve.wait_ge(step_done, 1)
            for mixed_t, col, done in ((xk_t, VC_MUK, xk_done), (xr_t, VC_MUR, xr_done)):
                for a in range(DH):
                    last = nc.vector.scalar_tensor_tensor(mixed_t[:, a, :], step_t[:, a, :], vec[:, col + a:col + a + 1],
                                                          shifted[:, a, 0:P], ALU.mult, ALU.add)
                last.then_inc(done, 1)
            dve.wait_ge(k_projected, 1)
            nc.vector.tensor_scalar(k_relu[:, :, :], ctx_turned_ps[:, :, 0:P], 0.0, None, ALU.max)\
                .then_inc(k_relu_done, 1)
            dve.wait_ge(r_projected, 1)
            nc.vector.tensor_scalar(gate_in[:, :], side_ps[:, 0:D], GATE_FLOOR, None, ALU.max).then_inc(gate_in_done, 1)
            dve.wait_ge(gate_exp_done, 1)
            nc.vector.tensor_scalar_add(gate_den[:, :], gate_exp[:, :], 1.0).then_inc(gate_den_done, 1)
            dve.wait_ge(gate_den_done, 1)
            nc.vector.reciprocal(gate[:, :], gate_den[:, :]).then_inc(gate_done, 1)
            dve.wait_ge(gate_done, 1)
            dve.wait_ge(mix_done, 1)
            nc.vector.tensor_tensor(out=mixed_out[:, :], in0=mixed_ps[:, 0:D], in1=gate[:, :], op=ALU.mult)\
                .then_inc(mixed_out_done, 1)
            dve.wait_ge(mixed_out_done, 1)
            nc.vector.tensor_tensor(out=x3[:, :], in0=mixed_out[:, :], in1=x2[:, :], op=ALU.add).then_inc(x3_done, 1)

        @block.tensor
        def _(pe):
            def turn(k, u):
                for t in range(tiles_of(k)):
                    for a in range(DH):
                        last = nc.tensor.transpose(ctx_turned_ps[:, a, t * P:(t + 1) * P],
                                                   ctx_rows[:, u, t, a * P:(a + 1) * P], ident)
                last.then_inc(ctx_turned, 1)

            def score(k, u):
                width = tiles_of(k) * P
                out_ps = scores_ps[:, u % 2, 0:width]
                pe.wait_ge(high_done, k * DH + DH)
                first = True
                for a in range(DH):
                    for q_part in (q_high, q_low):
                        nc.tensor.matmul(out_ps, q_part[:, a, :], ctx_high[:, u % 2, a, 0:width],
                                         start=first, stop=False)
                        first = False
                pe.wait_ge(low_done, k * DH + DH)
                for a in range(DH):
                    last = nc.tensor.matmul(out_ps, q_high[:, a, :], ctx_low[:, u % 2, a, 0:width],
                                            start=False, stop=(a == DH - 1))
                last.then_inc(scores_done, 1)

            def turn_probs(k, u):
                pe.wait_ge(exp_done, k + 1)
                for half in range(tiles_of(k) // 2):
                    for t in range(2):
                        col = (2 * half + t) * P
                        last = nc.tensor.transpose(probs_turned_ps[:, half, t * P:(t + 1) * P],
                                                   probs[:, u % 2, col:col + P], ident)
                    last.then_inc(probs_turned_done, 1)

            def mix(k, u):
                pe.wait_ge(acc_done, k + 1)
                tiles = tiles_of(k)
                for t in range(tiles):
                    if t % 2 == 0:
                        pe.wait_ge(probs_copied, 2 * k + (t // 2 + 1))
                    last = nc.tensor.matmul(mixed_ps[:, 0:D], probs_turned[:, u % 2, t, :], ctx_rows[:, u, t, :],
                                            start=(t == 0), stop=(t == tiles - 1))
                last.then_inc(mixed_done, 1)

            def features(kind, source, start=False, stop=False):
                for a in range(DH):
                    last = nc.tensor.matmul(hcq_ps, source[:, a, :], w[:, WB_QV + kind * DH + a, :],
                                            start=start and a == 0, stop=stop and a == DH - 1, skip_group_check=True)
                return last

            pe.wait_ge(const_loaded, 16)
            pe.wait_ge(ctx_loaded[0], 16)
            turn(0, 0)
            pe.wait_ge(normed_done, 1)
            for a in range(DH):
                last = nc.tensor.transpose(side_ps[:, a * P:(a + 1) * P], normed[:, 0, a * P:(a + 1) * P], ident)
            last.then_inc(normed_turned, 1)
            pe.wait_ge(low_done, DH)
            pe.wait_ge(ctx_loaded[1], 16)
            turn(1, 1)
            pe.wait_ge(q_high_done, 1)
            pe.wait_ge(q_low_done, 1)
            score(0, 0)
            with pe.Fori(0, LOOPED // RING) as turn_of_ring:
                base = turn_of_ring * RING
                for u in range(RING):
                    score(base + (u + 1), (u + 1) % RING)
                    turn_probs(base + u, u)
                    if u + 2 < RING:
                        pe.wait_ge(ctx_loaded[u + 2], turn_of_ring * 16 + 16)
                    else:
                        pe.wait_ge(ctx_loaded[u + 2 - RING], turn_of_ring * 16 + 32)
                    turn(base + (u + 2), (u + 2) % RING)
                    mix(base + u, u)
            for k in range(LOOPED, CHUNKS):
                if k + 1 < CHUNKS:
                    score(k + 1, (k + 1) % RING)
                turn_probs(k, k % RING)
                if k + 2 < CHUNKS:
                    pe.wait_ge(ctx_loaded[(k + 2) % RING], 16 * ((k + 2) // RING + 1))
                    turn(k + 2, (k + 2) % RING)
                if k == LOOPED:
                    pe.wait_ge(bias_loaded, 16)
                    pe.wait_ge(w_loaded, 16)
                    nc.tensor.matmul(hcq_ps, ones[0:1, :], bias[0:1, BR_QV:BR_QV + D], start=True, stop=False,
                                     skip_group_check=True)
                    for a in range(DH):
                        nc.tensor.matmul(side_ps[:, D:D + 1], normed_t[:, 0, a, :], vec[:, VC_W1 + a:VC_W1 + a + 1],
                                         start=False, stop=False, skip_group_check=True)
                    nc.tensor.matmul(side_ps[:, D:D + 1], ones[0:1, :], bias[0:1, BR_SIM:BR_SIM + 1],
                                     start=False, stop=True, skip_group_check=True).then_inc(hw1_done, 1)
                    features(0, normed_t[:, 0, :, :])
                mix(k, k % RING)
                if k == CHUNKS - 2:
                    pe.wait_ge(sim_max_done, 1)
                    nc.tensor.matmul(scores_ps[:, 1, 0:P], sim_max[:, 0:1].to_broadcast([P, P]), ident,
                                     start=True, stop=True).then_inc(sim_max_spread, 1)

            pe.wait_ge(batt_done, 1)
            for a in range(DH):
                nc.tensor.matmul(scores_ps[:, 0, a:a + 1], normed[:, 0, a * P:(a + 1) * P], batt[:, :],
                                 start=True, stop=True)
            nc.tensor.matmul(scores_ps[:, 0, DH:DH + 1], ones, batt[:, :], start=True, stop=True)\
                .then_inc(hc_bar_done, 1)
            pe.wait_ge(hq_done, 1)
            for a in range(DH):
                last = nc.tensor.transpose(probs_turned_ps[:, 0, a * P:(a + 1) * P], hq[:, a * P:(a + 1) * P], ident)
            last.then_inc(hq_turned, 1)
            pe.wait_ge(hc_hat_done, 1)
            features(3, hc_hat_t)
            pe.wait_ge(hq_t_done, 1)
            features(1, hq_t)
            pe.wait_ge(h_hq_done, 1)
            features(2, h_hq_t, stop=True).then_inc(hcq_done, 1)

            nc.tensor.matmul(scores_ps[:, 0, :], ones[0:1, :], bias[0:1, BR_Q:BR_Q + 2 * D], start=True, stop=False)
            nc.tensor.matmul(mixed_ps[:, 0:D], ones[0:1, :], bias[0:1, BR_V:BR_V + D], start=True, stop=False)
            pe.wait_ge(normed_done, 2)
            for a in range(DH):
                last = nc.tensor.transpose(probs_turned_ps[:, 0, a * P:(a + 1) * P], normed[:, 1, a * P:(a + 1) * P], ident)
            last.then_inc(normed_turned, 1)
            pe.wait_ge(normed_t_done, 2)
            for a in range(DH):
                last = nc.tensor.matmul(scores_ps[:, 0, :], normed_t[:, 1, a, :],
                                        w[:, WB_QK + 2 * a:WB_QK + 2 * a + 2, :], start=False, stop=(a == DH - 1))
            last.then_inc(qk_projected, 1)
            for a in range(DH):
                last = nc.tensor.matmul(mixed_ps[:, 0:D], normed_t[:, 1, a, :], w[:, WB_V + a, :],
                                        start=False, stop=(a == DH - 1))
            last.then_inc(v_projected, 1)
            nc.tensor.matmul(side_ps[:, D:2 * D], ones[0:1, :], bias[0:1, BR_O:BR_O + D], start=True, stop=False)
            pe.wait_ge(qk_done, 1)
            for a in range(DH):
                last = nc.tensor.transpose(probs_turned_ps[:, 0, a * P:(a + 1) * P], qk[:, a * P:(a + 1) * P], ident)
            last.then_inc(q_rot_turned, 1)
            pe.wait_ge(v_done, 1)
            for a in range(DH):
                last = nc.tensor.matmul(ctx_turned_ps[:, a, 0:P], qk[:, D + a * P:D + (a + 1) * P],
                                        v[:, a * P:(a + 1) * P], start=True, stop=True)
            last.then_inc(kv_done, 1)
            pe.wait_ge(q_rot_t_done, 1)
            pe.wait_ge(kv_masked, 1)
            for a in range(DH):
                last = nc.tensor.matmul(mixed_ps[:, a * P:(a + 1) * P], kv[:, a, :], q_rot_t[:, a, :],
                                        start=True, stop=True)
            last.then_inc(heads_done, 1)
            pe.wait_ge(heads_copied, 1)
            for a in range(DH):
                last = nc.tensor.matmul(side_ps[:, D:2 * D], heads_t[:, a, :], w[:, WB_O + a, :],
                                        start=False, stop=(a == DH - 1))
            last.then_inc(attn_done, 1)

            pe.wait_ge(normed_done, 3)
            for a in range(DH):
                last = nc.tensor.transpose(probs_turned_ps[:, 0, a * P:(a + 1) * P], normed[:, 2, a * P:(a + 1) * P], ident)
            last.then_inc(normed_turned, 1)
            pe.wait_ge(xk_done, 1)
            for b in range(DH):
                for a in range(DH):
                    last = nc.tensor.matmul(ctx_turned_ps[:, b, 0:P], w[:, WB_FK + a, b * P:(b + 1) * P], xk_t[:, a, :],
                                            start=(a == 0), stop=(a == DH - 1))
            last.then_inc(k_projected, 1)
            pe.wait_ge(xr_done, 1)
            for a in range(DH):
                last = nc.tensor.matmul(side_ps[:, 0:D], xr_t[:, a, :], w[:, WB_FR + a, :],
                                        start=(a == 0), stop=(a == DH - 1))
            last.then_inc(r_projected, 1)
            pe.wait_ge(k_act_done, 1)
            for a in range(DH):
                last = nc.tensor.matmul(mixed_ps[:, 0:D], k_act[:, a, :], w[:, WB_FV + a, :],
                                        start=(a == 0), stop=(a == DH - 1))
            last.then_inc(mix_done, 1)


def constants():
    c = np.zeros((P, C_ALL), np.float32)
    c[:, C_ID:C_ID + P] = np.eye(P, dtype=np.float32)
    head = np.arange(P) // HEAD_D
    c[:, C_MASK:C_MASK + P] = (head[:, None] == head[None, :]) * np.float32(HEAD_D ** -0.5)
    c[:, C_ONES:C_ONES + P] = 1.0
    power = np.arange(0, HEAD_D, 2).astype(np.float64)
    freqs = np.where(power < 10, 10000.0 ** -power, 0.0).astype(np.float32)
    angles = np.arange(L, dtype=np.float32)[:, None] * freqs[None, :]
    cos, sin = np.cos(angles), np.sin(angles)
    c[:, C_COS:C_COS + 2 * D] = np.tile(np.repeat(cos, 2, axis=1), (1, 2 * HEADS))
    c[:, C_SIN:C_SIN + 2 * D] = np.tile(np.stack([-sin, sin], axis=-1).reshape(L, HEAD_D), (1, 2 * HEADS))
    return c


def kernel(**inputs):
    import concourse.bacc as bacc
    from concourse.bass_utils import run_bass_kernel_spmd

    a = {name: np.asarray(value) for name, value in inputs.items()}

    def blocks(m):
        return [m[i:i + P] for i in range(0, m.shape[0], P)]

    wq, wk = blocks(a["L0_attn_Wq"]), blocks(a["L0_attn_Wk"])
    packed = blocks(a["L0_xattn_W_qv"]) + [wq[0], wk[0], wq[1], wk[1]] + blocks(a["L0_attn_Wv"]) \
        + blocks(a["L0_attn_Wo"]) + blocks(a["L0_ffn_W_k"].T) + blocks(a["L0_ffn_W_r"].T) + blocks(a["L0_ffn_W_v"].T)
    columns = [a["L0_xattn_w_sim"].reshape(3 * DH, P), a["L0_ffn_mu_r"].reshape(DH, P), a["L0_ffn_mu_k"].reshape(DH, P)]
    rows = [a["L0_xattn_b_qv"], a["L0_attn_bo"], a["L0_attn_bq"], a["L0_attn_bk"], a["L0_attn_bv"], a["L0_xattn_b_sim"]]
    arrays = {
        "x": a["x"].reshape(L, D),
        "ctx": a["ctx_1024"].reshape(S, D),
        "weights": np.concatenate(packed, axis=1),
        "vec": np.concatenate(columns, axis=0).T,
        "bias": np.concatenate(rows).reshape(1, BR),
        "const": constants(),
    }
    arrays = {name + "_dram": np.ascontiguousarray(value) for name, value in arrays.items()}

    nc = bacc.Bacc("TRN2", target_bir_lowering=False, num_devices=1)
    args = [nc.dram_tensor(name, value.shape, F32, kind="ExternalInput").ap() for name, value in arrays.items()]
    out = nc.dram_tensor("out_dram", (L, D), F32, kind="ExternalOutput").ap()
    build(nc, *args, out)
    result = run_bass_kernel_spmd(nc, [arrays], core_ids=[0])
    return result.results[0]["out_dram"].reshape(1, L, D)
```

```python
from contextlib import ExitStack

import numpy as np

import concourse.bass as bass
from concourse import mybir

P = 128
F32 = mybir.dt.float32
F32R = mybir.dt.float32r
BF16 = mybir.dt.bfloat16
ALU = mybir.AluOpType
ACT = mybir.ActivationFunctionType
AX_X = mybir.AxisListType.X

L = 128
D = 256
DH = D // P
HEADS = 16
HEAD_D = D // HEADS
S = 12544
TILES = 4
CHUNK = TILES * P
RING = 4
FULL = S // CHUNK
LAST_TILES = (S - FULL * CHUNK) // P
CHUNKS = FULL + 1
LOOPED = (FULL - RING) // RING * RING
EPS = 1e-5
GATE_FLOOR = -87.0
WARM_START, WARM_NORM_1, WARM_COPY, WARM_NORM_2, WARM_SHIFT = 8, 2, 2, 9, 6
FAR_BELOW = 3.0e38

WB_QV = 0
WB_Q = 4 * DH
WB_K = WB_Q + DH
WB_V = WB_K + DH
WB_O = WB_V + DH
WB_FK = WB_O + DH
WB_FR = WB_FK + DH
WB_FV = WB_FR + DH
WB = WB_FV + DH

VC_W1, VC_W2, VC_W3, VC_MUR, VC_MUK = (DH * n for n in range(5))
BR_QV, BR_O, BR_Q, BR_K, BR_V, BR_SIM = (D * n for n in range(6))
BR = 5 * D + 1
C_MASK, C_COS, C_SIN, C_ALL = 0, P, P + D, P + 2 * D


def build(nc, x, ctx_in, weights_in, vec_in, bias_in, const_in, out):
    ctx_full = ctx_in[0:FULL * CHUNK, :].rearrange("(k p t) d -> k p (t d)", p=P, t=TILES)
    ctx_last = ctx_in[FULL * CHUNK:S, :].rearrange("(p t) d -> p (t d)", t=LAST_TILES)

    with ExitStack() as stack:
        def sb(name, shape, dt=F32):
            return stack.enter_context(nc.sbuf_tensor(name, shape, dt))

        def ps(name, shape, dt=F32):
            return stack.enter_context(nc.psum_tensor(name, shape, dt))

        def sem(name):
            return stack.enter_context(nc.semaphore(name))

        const = sb("const", [P, C_ALL])
        block_mask = const[:, C_MASK:C_MASK + P]
        rope_cos = const[:, C_COS:C_COS + D]
        rope_sin = const[:, C_SIN:C_SIN + D]
        ident = sb("ident", [P, P])
        ones = sb("ones", [P, P])
        idle = sb("idle", [P, CHUNK], BF16)
        w = sb("w", [P, WB, D])
        vec = sb("vec", [P, 5 * DH])
        bias = sb("bias", [1, BR])
        x_sb = sb("x_sb", [P, D])
        ctx_rows = sb("ctx_rows", [P, RING, TILES, D])

        ctx_high = sb("ctx_high", [P, 2, DH, CHUNK], F32R)
        ctx_low = sb("ctx_low", [P, 2, DH, CHUNK], F32R)
        probs = sb("probs", [P, 2, CHUNK])
        rows_high = sb("rows_high", [P, RING, TILES, D], F32R)
        rows_low = sb("rows_low", [P, RING, TILES, D], F32R)
        turned_high = sb("turned_high", [P, 2, TILES, P], F32R)
        turned_low = sb("turned_low", [P, 2, TILES, P], F32R)
        unused = sb("unused", [P, CHUNK], BF16)
        neg_max = sb("neg_max", [P, RING])
        rescale = sb("rescale", [P, RING])
        row_sum = sb("row_sum", [P, RING])
        acc = sb("acc", [P, D])
        total = sb("total", [P, 1])

        ln_six = sb("ln_six", [P, 3, 6])
        ln_mv = sb("ln_mv", [P, 3, 2])
        ln_var = sb("ln_var", [P, 3])
        ln_rstd = sb("ln_rstd", [P, 3])
        minus_half = sb("minus_half", [P, 1])
        normed = sb("normed", [P, 3, D])
        normed_t = sb("normed_t", [P, 2, DH, P])
        q_t = sb("q_t", [P, DH, P])
        q_high = sb("q_high", [P, DH, P], F32R)
        q_low = sb("q_low", [P, DH, P], F32R)
        warm = sb("warm", [P, 1])

        hw1 = sb("hw1", [P, 1])
        sim_max = sb("sim_max", [P, 1])
        batt_neg_max = sb("batt_neg_max", [P, 1])
        batt = sb("batt", [P, 1])
        batt_inv = sb("batt_inv", [P, 1])
        hc_hat_t = sb("hc_hat_t", [P, DH, P])
        total_inv = sb("total_inv", [P, 1])
        acc_factor = sb("acc_factor", [P, 1])
        acc_scaled = sb("acc_scaled", [P, D])
        hq = sb("hq", [P, D])
        hq_t = sb("hq_t", [P, DH, P])
        h_hq_t = sb("h_hq_t", [P, DH, P])
        x1 = sb("x1", [P, D])

        with_cos = sb("with_cos", [P, 2, D])
        with_sin = sb("with_sin", [P, 2, D])
        rotated = sb("rotated", [P, 2, D])
        v = sb("v", [P, D])
        q_rot_t = sb("q_rot_t", [P, DH, P])
        kv = sb("kv", [P, DH, P])
        heads_t = sb("heads_t", [P, DH, P])
        x2 = sb("x2", [P, D])

        shifted = sb("shifted", [P, DH, P + 1])
        step_t = sb("step_t", [P, DH, P])
        xk_t = sb("xk_t", [P, DH, P])
        xr_t = sb("xr_t", [P, DH, P])
        k_relu = sb("k_relu", [P, DH, P])
        k_act = sb("k_act", [P, DH, P])
        gate_in = sb("gate_in", [P, D])
        gate_exp = sb("gate_exp", [P, D])
        gate_den = sb("gate_den", [P, D])
        gate = sb("gate", [P, D])
        mixed_out = sb("mixed_out", [P, D])
        x3 = sb("x3", [P, D])

        ctx_turned_ps = ps("ctx_turned_ps", [P, DH, CHUNK])
        scores_ps = ps("scores_ps", [P, 2, CHUNK])
        probs_turned_ps = ps("probs_turned_ps", [P, 2, CHUNK])
        mixed_ps = ps("mixed_ps", [P, CHUNK])
        side_ps = ps("side_ps", [P, CHUNK])
        hcq_ps = side_ps[:, 0:D]
        turn_ps = probs_turned_ps[:, 0, 0:D].rearrange("p (a l) -> p a l", a=DH)
        idle_ps = probs_turned_ps[:, 1, :]
        q_ps = scores_ps[:, 0, 0:D]
        k_ps = ctx_turned_ps[:, 0, 0:D]
        v_ps = mixed_ps[:, 0:D]
        kv_ps = ctx_turned_ps[:, 1, 0:D].rearrange("p (a l) -> p a l", a=DH)
        heads_ps = side_ps[:, 0:D].rearrange("p (a l) -> p a l", a=DH)
        x2_ps = scores_ps[:, 1, 0:D]
        r_ps = ctx_turned_ps[:, 0, 0:D]
        k_t_ps = (scores_ps[:, 0, 0:P], ctx_turned_ps[:, 1, 0:P])
        mix_ps = mixed_ps[:, 0:D]

        x_loaded = sem("x_loaded")
        const_loaded = sem("const_loaded")
        vec_loaded = sem("vec_loaded")
        bias_loaded = sem("bias_loaded")
        w_qv_loaded = sem("w_qv_loaded")
        w_loaded = sem("w_loaded")
        ident_zeroed = sem("ident_zeroed")
        ident_done = sem("ident_done")
        idle_zeroed = sem("idle_zeroed")
        ones_set = sem("ones_set")
        ctx_loaded = [sem(f"ctx_loaded{r}") for r in range(RING)]
        out_stored = sem("out_stored")

        minus_half_set = sem("minus_half_set")
        shift_zeroed = sem("shift_zeroed")
        stats_done = sem("stats_done")
        mv_done = sem("mv_done")
        var_done = sem("var_done")
        rstd_done = sem("rstd_done")
        normed_done = sem("normed_done")
        normed_turned = sem("normed_turned")
        normed_t_done = sem("normed_t_done")
        q_done = sem("q_done")
        q_high_done = sem("q_high_done")
        q_low_done = sem("q_low_done")

        ctx_turned = sem("ctx_turned")
        high_done = sem("high_done")
        low_done = sem("low_done")
        scores_done = sem("scores_done")
        max_done = sem("max_done")
        exp_done = sem("exp_done")
        rescale_done = sem("rescale_done")
        probs_turned_done = sem("probs_turned_done")
        probs_high_done = sem("probs_high_done")
        probs_low_done = sem("probs_low_done")
        rows_high_done = sem("rows_high_done")
        rows_low_done = sem("rows_low_done")
        mixed_done = sem("mixed_done")
        acc_done = sem("acc_done")
        total_done = sem("total_done")

        hw1_done = sem("hw1_done")
        factor_done = sem("factor_done")
        acc_scaled_done = sem("acc_scaled_done")
        sim_max_done = sem("sim_max_done")
        sim_max_spread = sem("sim_max_spread")
        batt_max_done = sem("batt_max_done")
        batt_done = sem("batt_done")
        hc_bar_done = sem("hc_bar_done")
        batt_inv_done = sem("batt_inv_done")
        hc_hat_done = sem("hc_hat_done")
        total_inv_done = sem("total_inv_done")
        hq_done = sem("hq_done")
        hq_turned = sem("hq_turned")
        hq_t_done = sem("hq_t_done")
        h_hq_done = sem("h_hq_done")
        hcq_done = sem("hcq_done")
        x1_done = sem("x1_done")

        q_projected = sem("q_projected")
        k_rows_projected = sem("k_rows_projected")
        v_projected = sem("v_projected")
        cos_done = sem("cos_done")
        sin_done = sem("sin_done")
        rotated_done = sem("rotated_done")
        v_done = sem("v_done")
        q_rot_turned = sem("q_rot_turned")
        q_rot_t_done = sem("q_rot_t_done")
        kv_done = sem("kv_done")
        kv_masked = sem("kv_masked")
        heads_done = sem("heads_done")
        heads_copied = sem("heads_copied")
        attn_done = sem("attn_done")
        x2_done = sem("x2_done")

        step_done = sem("step_done")
        xk_done = sem("xk_done")
        xr_done = sem("xr_done")
        k_projected = sem("k_projected")
        r_projected = sem("r_projected")
        k_relu_done = sem("k_relu_done")
        k_act_done = sem("k_act_done")
        gate_in_done = sem("gate_in_done")
        gate_exp_done = sem("gate_exp_done")
        gate_den_done = sem("gate_den_done")
        gate_done = sem("gate_done")
        mix_done = sem("mix_done")
        mixed_out_done = sem("mixed_out_done")
        x3_done = sem("x3_done")

        block = stack.enter_context(nc.Block())

        def tiles_of(k):
            return LAST_TILES if isinstance(k, int) and k == CHUNKS - 1 else TILES

        @block.sync
        def _(sp):
            sp.dma_start(x_sb[:, :], x).then_inc(x_loaded, 16)
            for k in range(RING):
                sp.dma_start(ctx_rows[:, k, :, :], ctx_full[k].rearrange("p (t d) -> p t d", t=TILES))\
                    .then_inc(ctx_loaded[k], 16)
            with sp.Fori(0, (FULL - RING) // RING) as turn_of_ring:
                base = turn_of_ring * RING
                for u in range(RING):
                    sp.wait_ge(ctx_turned, base + (u + 1))
                    sp.wait_ge(rows_low_done, base + (u + 1))
                    src = ctx_full[bass.ds(base + (u + RING), 1), :, :]
                    sp.dma_start(ctx_rows[:, u, :, :], src.rearrange("k p (t d) -> p (k t) d", t=TILES))\
                        .then_inc(ctx_loaded[u], 16)
            k = CHUNKS - 1
            sp.wait_ge(ctx_turned, k - RING + 1)
            sp.wait_ge(rows_low_done, k - RING + 1)
            sp.dma_start(ctx_rows[:, k % RING, 0:LAST_TILES, :],
                         ctx_last.rearrange("p (t d) -> p t d", t=LAST_TILES)).then_inc(ctx_loaded[k % RING], 16)
            blocks_in = weights_in.rearrange("p (b n) -> p b n", b=WB)
            sp.dma_start(w[:, 0:WB_Q, :], blocks_in[:, 0:WB_Q, :]).then_inc(w_qv_loaded, 16)
            sp.dma_start(w[:, WB_Q:WB, :], blocks_in[:, WB_Q:WB, :]).then_inc(w_loaded, 16)
            sp.dma_start(const[:, :], const_in).then_inc(const_loaded, 16)
            sp.wait_ge(x3_done, 1)
            sp.dma_start(out, x3[:, :]).then_inc(out_stored, 16)
            sp.wait_ge(out_stored, 16)

        @block.gpsimd
        def _(pool):
            nc.gpsimd.memset(minus_half[:, :], -0.5).then_inc(minus_half_set, 1)
            nc.gpsimd.memset(ident[:, :], 0.0).then_inc(ident_zeroed, 1)
            pool.wait_ge(ident_zeroed, 1)
            nc.gpsimd.affine_select(out=ident[:, :], in_=ident[:, :], compare_op=ALU.not_equal, fill=1.0, base=0,
                                    pattern=[[-1, P]], channel_multiplier=1).then_inc(ident_done, 1)
            nc.gpsimd.memset(shifted[:, :, 0:1], 0.0).then_inc(shift_zeroed, 1)
            pool.wait_ge(minus_half_set, 1)

            def power(n):
                pool.wait_ge(var_done, n + 1)
                nc.gpsimd.tensor_tensor(out=ln_rstd[:, n:n + 1], in0=ln_var[:, n:n + 1], in1=minus_half[:, :],
                                        op=ALU.pow).then_inc(rstd_done, 1)

            def take_rows_low(k, u):
                tiles = tiles_of(k)
                pool.wait_ge(rows_high_done, k + 1)
                nc.gpsimd.tensor_tensor(out=rows_low[:, u, 0:tiles, :], in0=ctx_rows[:, u, 0:tiles, :],
                                        in1=rows_high[:, u, 0:tiles, :].bitcast(F32), op=ALU.subtract)\
                    .then_inc(rows_low_done, 1)

            power(0)
            for k in range(2):
                take_rows_low(k, k)
            with pool.Fori(0, LOOPED // RING) as turn_of_ring:
                base = turn_of_ring * RING
                for u in range(RING):
                    take_rows_low(base + (u + 2), (u + 2) % RING)
            for k in range(LOOPED + 2, CHUNKS):
                take_rows_low(k, k % RING)
            power(1)
            power(2)

        @block.scalar
        def _(act):
            act.wait_ge(minus_half_set, 1)
            nc.scalar.activation(warm[:, :], minus_half[:, :], ACT.Exp)
            act.dma_start(vec[:, :], vec_in).then_inc(vec_loaded, 16)
            act.dma_start(bias[:, :], bias_in).then_inc(bias_loaded, 16)

            def take_high(k, u, turned=ctx_turned_ps):
                width = tiles_of(k) * P
                act.wait_ge(ctx_turned, k + 1)
                for a in range(DH):
                    nc.scalar.activation(ctx_high[:, u % 2, a, 0:width], turned[:, a, 0:width],
                                         ACT.Copy).then_inc(high_done, 1)

            def exps(k, u):
                width = tiles_of(k) * P
                act.wait_ge(max_done, k + 2)
                nc.scalar.activation(probs[:, u % 2, 0:width], scores_ps[:, u % 2, 0:width], ACT.Exp,
                                     bias=neg_max[:, u:u + 1], accum_out=row_sum[:, u:u + 1])\
                    .then_inc(exp_done, 1)
                before = (u - 1) % RING
                nc.scalar.activation(rescale[:, u:u + 1], neg_max[:, before:before + 1], ACT.Exp,
                                     bias=neg_max[:, u:u + 1], scale=-1.0).then_inc(rescale_done, 1)

            def probs_high(k, u):
                for half in range(tiles_of(k) // 2):
                    act.wait_ge(probs_turned_done, 2 * k + (half + 1))
                    nc.scalar.activation(turned_high[:, u % 2, 2 * half:2 * half + 2, :],
                                         probs_turned_ps[:, half, 0:2 * P].rearrange("p (t l) -> p t l", t=2),
                                         ACT.Copy).then_inc(probs_high_done, 1)

            def take_rows_high(k, u):
                tiles = tiles_of(k)
                nc.scalar.activation(rows_high[:, u, 0:tiles, :], ctx_rows[:, u, 0:tiles, :], ACT.Copy)\
                    .then_inc(rows_high_done, 1)

            take_high(0, 0)
            act.wait_ge(q_done, 1)
            nc.scalar.activation(q_high[:, :, :], q_t[:, :, :], ACT.Copy).then_inc(q_high_done, 1)
            take_high(1, 1, probs_turned_ps)
            act.wait_ge(ctx_loaded[0], 16)
            take_rows_high(0, 0)
            act.wait_ge(q_done, 1)
            nc.scalar.activation(normed_t[:, 0, :, :], side_ps[:, 0:D].rearrange("p (a l) -> p a l", a=DH),
                                 ACT.Copy).then_inc(normed_t_done, 1)
            exps(0, 0)
            act.wait_ge(ctx_loaded[1], 16)
            take_rows_high(1, 1)
            with act.Fori(0, LOOPED // RING) as turn_of_ring:
                base = turn_of_ring * RING
                for u in range(RING):
                    probs_high(base + u, u)
                    take_high(base + (u + 2), (u + 2) % RING)
                    exps(base + (u + 1), (u + 1) % RING)
                    if u + 2 < RING:
                        act.wait_ge(ctx_loaded[u + 2], turn_of_ring * 16 + 16)
                    else:
                        act.wait_ge(ctx_loaded[u + 2 - RING], turn_of_ring * 16 + 32)
                    take_rows_high(base + (u + 2), (u + 2) % RING)
            for k in range(LOOPED, CHUNKS):
                probs_high(k, k % RING)
                if k + 2 < CHUNKS:
                    take_high(k + 2, (k + 2) % RING)
                if k + 1 < CHUNKS:
                    exps(k + 1, (k + 1) % RING)
                if k + 2 < CHUNKS:
                    act.wait_ge(ctx_loaded[(k + 2) % RING], 16 * ((k + 2) // RING + 1))
                    take_rows_high(k + 2, (k + 2) % RING)

            act.wait_ge(batt_max_done, 1)
            nc.scalar.activation(batt[:, :], sim_max[:, :], ACT.Exp, bias=batt_neg_max[:, :]).then_inc(batt_done, 1)
            act.wait_ge(hq_turned, 1)
            nc.scalar.activation(hq_t[:, :, :], turn_ps, ACT.Copy).then_inc(hq_t_done, 1)

            act.wait_ge(normed_done, 2)
            nc.scalar.activation(x1[:, :], hcq_ps, ACT.Copy).then_inc(x1_done, 1)
            act.wait_ge(normed_turned, 2)
            nc.scalar.activation(normed_t[:, 1, :, :], turn_ps, ACT.Copy).then_inc(normed_t_done, 1)
            act.wait_ge(q_rot_turned, 1)
            nc.scalar.activation(q_rot_t[:, :, :], turn_ps, ACT.Copy).then_inc(q_rot_t_done, 1)
            act.wait_ge(v_projected, 1)
            nc.scalar.activation(v[:, :], v_ps, ACT.Copy).then_inc(v_done, 1)
            act.wait_ge(heads_done, 1)
            nc.scalar.activation(heads_t[:, :, :], heads_ps, ACT.Copy).then_inc(heads_copied, 1)

            act.wait_ge(normed_done, 3)
            nc.scalar.activation(x2[:, :], x2_ps, ACT.Copy).then_inc(x2_done, 1)
            act.wait_ge(shift_zeroed, 1)
            act.wait_ge(normed_turned, 3)
            nc.scalar.activation(shifted[:, :, 1:P + 1], turn_ps, ACT.Copy).then_inc(normed_t_done, 1)
            act.wait_ge(gate_in_done, 1)
            nc.scalar.activation(gate_exp[:, :], gate_in[:, :], ACT.Exp, scale=-1.0).then_inc(gate_exp_done, 1)
            for b in range(DH):
                act.wait_ge(k_relu_done, b + 1)
                nc.scalar.activation(k_act[:, b, :], k_relu[:, b, :], ACT.Square).then_inc(k_act_done, 1)

        @block.vector
        def _(dve):
            def layer_norm(n, source):
                nc.vector.bn_stats(ln_six[:, n, :], source).then_inc(stats_done, 1)
                dve.wait_ge(stats_done, n + 1)
                nc.vector.bn_aggr(ln_mv[:, n, :], ln_six[:, n, :]).then_inc(mv_done, 1)
                dve.wait_ge(mv_done, n + 1)
                nc.vector.tensor_scalar_add(ln_var[:, n:n + 1], ln_mv[:, n, 1:2], EPS).then_inc(var_done, 1)
                dve.wait_ge(rstd_done, n + 1)
                nc.vector.tensor_scalar(normed[:, n, :], source, ln_mv[:, n, 0:1], ln_rstd[:, n:n + 1],
                                        ALU.subtract, ALU.mult).then_inc(normed_done, 1)

            def take_low(k, u, turned=ctx_turned_ps, halves=range(DH)):
                width = tiles_of(k) * P
                for a in halves:
                    dve.wait_ge(high_done, k * DH + (a + 1))
                    nc.vector.tensor_tensor(out=ctx_low[:, u % 2, a, 0:width], in0=turned[:, a, 0:width],
                                            in1=ctx_high[:, u % 2, a, 0:width].bitcast(F32), op=ALU.subtract)\
                        .then_inc(low_done, 1)

            def running_max(k, u):
                width = tiles_of(k) * P
                before = (u - 1) % RING
                dve.wait_ge(scores_done, k + 1)
                dve.wait_ge(max_done, k + 1)
                nc.vector.tensor_scalar(unused[:, 0:width], scores_ps[:, u % 2, 0:width], -1.0,
                                        neg_max[:, before:before + 1], ALU.mult, ALU.min,
                                        accum_out=neg_max[:, u:u + 1]).then_inc(max_done, 1)

            def probs_low(k, u):
                for half in range(tiles_of(k) // 2):
                    dve.wait_ge(probs_high_done, 2 * k + (half + 1))
                    nc.vector.tensor_tensor(out=turned_low[:, u % 2, 2 * half:2 * half + 2, :],
                                            in0=probs_turned_ps[:, half, 0:2 * P].rearrange("p (t l) -> p t l", t=2),
                                            in1=turned_high[:, u % 2, 2 * half:2 * half + 2, :].bitcast(F32),
                                            op=ALU.subtract).then_inc(probs_low_done, 1)

            def add_total(k, u):
                dve.wait_ge(exp_done, k + 1)
                dve.wait_ge(rescale_done, k + 1)
                dve.wait_ge(total_done, k + 1)
                nc.vector.scalar_tensor_tensor(total[:, :], total[:, :], rescale[:, u:u + 1], row_sum[:, u:u + 1],
                                               ALU.mult, ALU.add).then_inc(total_done, 1)

            def accumulate(k, u):
                add_total(k, u)
                dve.wait_ge(mixed_done, k + 1)
                if isinstance(k, int) and k == LOOPED:
                    nc.vector.tensor_copy(hw1[:, :], mixed_ps[:, D:D + 1]).then_inc(hw1_done, 1)
                dve.wait_ge(acc_done, k + 1)
                nc.vector.scalar_tensor_tensor(acc[:, :], acc[:, :], rescale[:, u:u + 1], mixed_ps[:, 0:D],
                                               ALU.mult, ALU.add).then_inc(acc_done, 1)

            nc.vector.memset(idle[:, :], 0.0).then_inc(idle_zeroed, 1)
            nc.vector.memset(neg_max[:, RING - 1:RING], FAR_BELOW).then_inc(max_done, 1)
            nc.vector.memset(acc[:, :], 0.0).then_inc(acc_done, 1)
            nc.vector.memset(total[:, :], 0.0).then_inc(total_done, 1)
            nc.vector.memset(ones[:, :], 1.0).then_inc(ones_set, 1)
            dve.wait_ge(x_loaded, 16)
            layer_norm(0, x_sb[:, :])
            dve.wait_ge(vec_loaded, 16)
            dve.wait_ge(normed_turned, 1)
            for a in range(DH):
                last = nc.vector.tensor_scalar(q_t[:, a, :], side_ps[:, a * P:(a + 1) * P],
                                               vec[:, VC_W3 + a:VC_W3 + a + 1], vec[:, VC_W2 + a:VC_W2 + a + 1],
                                               ALU.mult, ALU.add)
            last.then_inc(q_done, 1)
            take_low(0, 0, halves=[0])
            dve.wait_ge(q_high_done, 1)
            nc.vector.tensor_tensor(out=q_low[:, :, :], in0=q_t[:, :, :], in1=q_high[:, :, :].bitcast(F32),
                                    op=ALU.subtract).then_inc(q_low_done, 1)
            take_low(0, 0, halves=[1])
            take_low(1, 1, probs_turned_ps, halves=[0])
            running_max(0, 0)
            take_low(1, 1, probs_turned_ps, halves=[1])
            with dve.Fori(0, LOOPED // RING) as turn_of_ring:
                base = turn_of_ring * RING
                for u in range(RING):
                    probs_low(base + u, u)
                    running_max(base + (u + 1), (u + 1) % RING)
                    take_low(base + (u + 2), (u + 2) % RING)
                    accumulate(base + u, u)
            for k in range(LOOPED, CHUNKS - 1):
                probs_low(k, k % RING)
                running_max(k + 1, (k + 1) % RING)
                if k + 2 < CHUNKS:
                    take_low(k + 2, (k + 2) % RING)
                else:
                    u = (k + 1) % RING
                    dve.wait_ge(hw1_done, 1)
                    dve.wait_ge(max_done, CHUNKS + 1)
                    nc.vector.tensor_tensor(out=sim_max[:, :], in0=hw1[:, :], in1=neg_max[:, u:u + 1],
                                            op=ALU.subtract).then_inc(sim_max_done, 1)
                accumulate(k, k % RING)
            k, u = CHUNKS - 1, (CHUNKS - 1) % RING
            dve.wait_ge(sim_max_spread, 1)
            nc.vector.tensor_reduce(batt_neg_max[:, :], scores_ps[:, 1, 0:P], axis=AX_X, op=ALU.max,
                                    negate=True).then_inc(batt_max_done, 1)
            probs_low(k, u)
            add_total(k, u)
            dve.wait_ge(total_done, CHUNKS + 1)
            nc.vector.reciprocal(total_inv[:, :], total[:, :]).then_inc(total_inv_done, 1)
            dve.wait_ge(hc_bar_done, 1)
            nc.vector.reciprocal(batt_inv[:, :], scores_ps[:, 0, DH:DH + 1]).then_inc(batt_inv_done, 1)
            dve.wait_ge(total_inv_done, 1)
            nc.vector.tensor_tensor(out=acc_factor[:, :], in0=total_inv[:, :], in1=rescale[:, u:u + 1],
                                    op=ALU.mult).then_inc(factor_done, 1)
            dve.wait_ge(batt_inv_done, 1)
            dve.wait_ge(normed_t_done, 1)
            for a in range(DH):
                last = nc.vector.tensor_scalar(hc_hat_t[:, a, :], normed_t[:, 0, a, :], scores_ps[:, 0, a:a + 1],
                                               batt_inv[:, :], ALU.mult, ALU.mult)
            last.then_inc(hc_hat_done, 1)
            dve.wait_ge(factor_done, 1)
            dve.wait_ge(acc_done, CHUNKS)
            nc.vector.tensor_scalar(acc_scaled[:, :], acc[:, :], acc_factor[:, :], None, ALU.mult)\
                .then_inc(acc_scaled_done, 1)
            dve.wait_ge(acc_scaled_done, 1)
            dve.wait_ge(mixed_done, CHUNKS)
            nc.vector.scalar_tensor_tensor(hq[:, :], mixed_ps[:, 0:D], total_inv[:, :], acc_scaled[:, :],
                                           ALU.mult, ALU.add).then_inc(hq_done, 1)
            dve.wait_ge(hq_t_done, 1)
            nc.vector.tensor_tensor(out=h_hq_t[:, :, :], in0=normed_t[:, 0, :, :], in1=hq_t[:, :, :],
                                    op=ALU.mult).then_inc(h_hq_done, 1)

            dve.wait_ge(hcq_done, 1)
            layer_norm(1, hcq_ps)
            dve.wait_ge(const_loaded, 16)
            for n, (part_ps, projected) in enumerate(((q_ps, q_projected), (k_ps, k_rows_projected))):
                dve.wait_ge(projected, 1)
                nc.vector.tensor_tensor(out=with_cos[:, n, :], in0=part_ps, in1=rope_cos, op=ALU.mult)\
                    .then_inc(cos_done, 1)
                nc.vector.tensor_tensor(out=with_sin[:, n, :].rearrange("p (m c) -> p m c", c=2),
                                        in0=part_ps.rearrange("p (m c) -> p m c", c=2)[:, :, ::-1],
                                        in1=rope_sin.rearrange("p (m c) -> p m c", c=2), op=ALU.mult)\
                    .then_inc(sin_done, 1)
                dve.wait_ge(cos_done, n + 1)
                dve.wait_ge(sin_done, n + 1)
                nc.vector.tensor_tensor(out=rotated[:, n, :], in0=with_cos[:, n, :], in1=with_sin[:, n, :],
                                        op=ALU.add).then_inc(rotated_done, 1)
            dve.wait_ge(kv_done, 1)
            nc.vector.tensor_tensor(out=kv[:, :, :], in0=kv_ps, in1=block_mask.unsqueeze(1).to_broadcast([P, DH, P]),
                                    op=ALU.mult).then_inc(kv_masked, 1)

            dve.wait_ge(attn_done, 1)
            layer_norm(2, x2_ps)
            dve.wait_ge(normed_t_done, 3)
            nc.vector.tensor_tensor(out=step_t[:, :, :], in0=shifted[:, :, 1:P + 1], in1=shifted[:, :, 0:P],
                                    op=ALU.subtract).then_inc(step_done, 1)
            dve.wait_ge(step_done, 1)
            for mixed_t, col, done in ((xr_t, VC_MUR, xr_done), (xk_t, VC_MUK, xk_done)):
                for a in range(DH):
                    last = nc.vector.scalar_tensor_tensor(mixed_t[:, a, :], step_t[:, a, :], vec[:, col + a:col + a + 1],
                                                          shifted[:, a, 0:P], ALU.mult, ALU.add)
                last.then_inc(done, 1)
            dve.wait_ge(r_projected, 1)
            nc.vector.tensor_scalar(gate_in[:, :], r_ps, GATE_FLOOR, None, ALU.max).then_inc(gate_in_done, 1)
            for b in range(DH):
                dve.wait_ge(k_projected, b + 1)
                nc.vector.tensor_scalar(k_relu[:, b, :], k_t_ps[b], 0.0, None, ALU.max).then_inc(k_relu_done, 1)
            dve.wait_ge(gate_exp_done, 1)
            nc.vector.tensor_scalar_add(gate_den[:, :], gate_exp[:, :], 1.0).then_inc(gate_den_done, 1)
            dve.wait_ge(gate_den_done, 1)
            nc.vector.reciprocal(gate[:, :], gate_den[:, :]).then_inc(gate_done, 1)
            dve.wait_ge(gate_done, 1)
            dve.wait_ge(mix_done, 1)
            nc.vector.tensor_tensor(out=mixed_out[:, :], in0=mix_ps, in1=gate[:, :], op=ALU.mult)\
                .then_inc(mixed_out_done, 1)
            dve.wait_ge(mixed_out_done, 1)
            dve.wait_ge(x2_done, 1)
            nc.vector.tensor_tensor(out=x3[:, :], in0=mixed_out[:, :], in1=x2[:, :], op=ALU.add).then_inc(x3_done, 1)

        @block.tensor
        def _(pe):
            def keep_warm(n):
                for _ in range(n):
                    nc.tensor.matmul(idle_ps, idle[:, 0:P], idle[:, :], start=True, stop=True)

            def turn_square(source):
                for a in range(DH):
                    last = nc.tensor.transpose(turn_ps[:, a, :], source[:, a * P:(a + 1) * P], ident[:, :])
                return last

            def add_bias(out_ps, col):
                nc.tensor.matmul(out_ps, ones[0:1, :], bias[0:1, col:col + D], start=True, stop=False)

            def turn(k, u, turned=ctx_turned_ps):
                for t in range(tiles_of(k)):
                    for a in range(DH):
                        last = nc.tensor.transpose(turned[:, a, t * P:(t + 1) * P],
                                                   ctx_rows[:, u, t, a * P:(a + 1) * P], ident[:, :])
                last.then_inc(ctx_turned, 1)

            def score(k, u):
                width = tiles_of(k) * P
                out_ps = scores_ps[:, u % 2, 0:width]
                def product(a, q_part, c_part, first=False, end=False):
                    return nc.tensor.matmul(out_ps, q_part[:, a, :], c_part[:, u % 2, a, 0:width], start=first, stop=end)

                for a in range(DH):
                    pe.wait_ge(high_done, k * DH + (a + 1))
                    product(a, q_high, ctx_high, first=(a == 0))
                if isinstance(k, int) and k == 0:
                    pe.wait_ge(q_low_done, 1)
                for a in range(DH):
                    product(a, q_low, ctx_high)
                for a in range(DH):
                    pe.wait_ge(low_done, k * DH + (a + 1))
                    last = product(a, q_high, ctx_low, end=(a == DH - 1))
                last.then_inc(scores_done, 1)

            def turn_probs(k, u):
                pe.wait_ge(exp_done, k + 1)
                for half in range(tiles_of(k) // 2):
                    for t in range(2):
                        col = (2 * half + t) * P
                        last = nc.tensor.transpose(probs_turned_ps[:, half, t * P:(t + 1) * P],
                                                   probs[:, u % 2, col:col + P], ident[:, :])
                    last.then_inc(probs_turned_done, 1)

            def mix(k, u):
                pe.wait_ge(acc_done, k + 1)
                if isinstance(k, int) and k == LOOPED:
                    for a in range(DH):
                        nc.tensor.matmul(mixed_ps[:, D:D + 1], normed_t[:, 0, a, :], vec[:, VC_W1 + a:VC_W1 + a + 1],
                                         start=(a == 0), stop=False)
                    nc.tensor.matmul(mixed_ps[:, D:D + 1], ones[0:1, :], bias[0:1, BR_SIM:BR_SIM + 1],
                                     start=False, stop=True)
                tiles = tiles_of(k)
                pe.wait_ge(rows_low_done, k + 1)
                for t in range(tiles):
                    if t % 2 == 0:
                        pe.wait_ge(probs_low_done, 2 * k + (t // 2 + 1))
                    for probs_part, rows_part in ((turned_high, rows_high), (turned_high, rows_low),
                                                  (turned_low, rows_high)):
                        last = nc.tensor.matmul(mixed_ps[:, 0:D], probs_part[:, u % 2, t, :], rows_part[:, u, t, :],
                                                start=(t == 0 and rows_part is rows_high and probs_part is turned_high),
                                                stop=(t == tiles - 1 and probs_part is turned_low))
                last.then_inc(mixed_done, 1)

            def features(kind, source, stop=False):
                for a in range(DH):
                    last = nc.tensor.matmul(hcq_ps, source[:, a, :], w[:, WB_QV + kind * DH + a, :],
                                            start=False, stop=stop and a == DH - 1)
                return last

            pe.wait_ge(idle_zeroed, 1)
            keep_warm(WARM_START)
            pe.wait_ge(ident_done, 1)
            pe.wait_ge(ctx_loaded[0], 16)
            turn(0, 0)
            pe.wait_ge(normed_done, 1)
            for a in range(DH):
                last = nc.tensor.transpose(side_ps[:, a * P:(a + 1) * P], normed[:, 0, a * P:(a + 1) * P], ident[:, :])
            last.then_inc(normed_turned, 1)
            pe.wait_ge(ctx_loaded[1], 16)
            turn(1, 1, probs_turned_ps)
            pe.wait_ge(q_high_done, 1)
            score(0, 0)
            with pe.Fori(0, LOOPED // RING) as turn_of_ring:
                base = turn_of_ring * RING
                for u in range(RING):
                    score(base + (u + 1), (u + 1) % RING)
                    turn_probs(base + u, u)
                    if u + 2 < RING:
                        pe.wait_ge(ctx_loaded[u + 2], turn_of_ring * 16 + 16)
                    else:
                        pe.wait_ge(ctx_loaded[u + 2 - RING], turn_of_ring * 16 + 32)
                    turn(base + (u + 2), (u + 2) % RING)
                    mix(base + u, u)
            pe.wait_ge(ones_set, 1)
            pe.wait_ge(bias_loaded, 16)
            pe.wait_ge(normed_t_done, 1)
            for k in range(LOOPED, CHUNKS - 1):
                score(k + 1, (k + 1) % RING)
                turn_probs(k, k % RING)
                if k + 2 < CHUNKS:
                    pe.wait_ge(ctx_loaded[(k + 2) % RING], 16 * ((k + 2) // RING + 1))
                    turn(k + 2, (k + 2) % RING)
                else:
                    pe.wait_ge(w_qv_loaded, 16)
                    add_bias(hcq_ps, BR_QV)
                    features(0, normed_t[:, 0, :, :])
                mix(k, k % RING)
            pe.wait_ge(sim_max_done, 1)
            nc.tensor.matmul(scores_ps[:, 1, 0:P], sim_max[:, 0:1].to_broadcast([P, P]), ident[:, :],
                             start=True, stop=True).then_inc(sim_max_spread, 1)
            turn_probs(CHUNKS - 1, (CHUNKS - 1) % RING)
            nc.tensor.matmul(hcq_ps, ident[:, :], x_sb[:, :], start=False, stop=False)
            pe.wait_ge(batt_done, 1)
            for a in range(DH):
                nc.tensor.matmul(scores_ps[:, 0, a:a + 1], normed[:, 0, a * P:(a + 1) * P], batt[:, :],
                                 start=True, stop=True)
            nc.tensor.matmul(scores_ps[:, 0, DH:DH + 1], ones[:, :], batt[:, :], start=True, stop=True)\
                .then_inc(hc_bar_done, 1)
            mix(CHUNKS - 1, (CHUNKS - 1) % RING)
            pe.wait_ge(hc_hat_done, 1)
            features(3, hc_hat_t)
            pe.wait_ge(hq_done, 1)
            turn_square(hq).then_inc(hq_turned, 1)
            pe.wait_ge(hq_t_done, 1)
            features(1, hq_t)
            pe.wait_ge(h_hq_done, 1)
            features(2, h_hq_t, stop=True).then_inc(hcq_done, 1)

            for out_ps, col in ((q_ps, BR_Q), (k_ps, BR_K), (v_ps, BR_V), (x2_ps, BR_O)):
                add_bias(out_ps, col)
            pe.wait_ge(w_loaded, 16)
            keep_warm(WARM_NORM_1)
            pe.wait_ge(normed_done, 2)
            turn_square(normed[:, 1, :]).then_inc(normed_turned, 1)
            keep_warm(WARM_COPY)
            pe.wait_ge(normed_t_done, 2)
            for out_ps, block_row, done in ((q_ps, WB_Q, q_projected), (k_ps, WB_K, k_rows_projected),
                                            (v_ps, WB_V, v_projected)):
                for a in range(DH):
                    last = nc.tensor.matmul(out_ps, normed_t[:, 1, a, :], w[:, block_row + a, :],
                                            start=False, stop=(a == DH - 1))
                last.then_inc(done, 1)
            pe.wait_ge(x1_done, 1)
            nc.tensor.matmul(x2_ps, ident[:, :], x1[:, :], start=False, stop=False)
            pe.wait_ge(rotated_done, 1)
            turn_square(rotated[:, 0, :]).then_inc(q_rot_turned, 1)
            pe.wait_ge(rotated_done, 2)
            pe.wait_ge(v_done, 1)
            for a in range(DH):
                last = nc.tensor.matmul(kv_ps[:, a, :], rotated[:, 1, a * P:(a + 1) * P], v[:, a * P:(a + 1) * P],
                                        start=True, stop=True)
            last.then_inc(kv_done, 1)
            pe.wait_ge(q_rot_t_done, 1)
            pe.wait_ge(kv_masked, 1)
            for a in range(DH):
                last = nc.tensor.matmul(heads_ps[:, a, :], kv[:, a, :], q_rot_t[:, a, :], start=True, stop=True)
            last.then_inc(heads_done, 1)
            pe.wait_ge(heads_copied, 1)
            for a in range(DH):
                last = nc.tensor.matmul(x2_ps, heads_t[:, a, :], w[:, WB_O + a, :], start=False, stop=(a == DH - 1))
            last.then_inc(attn_done, 1)

            keep_warm(WARM_NORM_2)
            pe.wait_ge(normed_done, 3)
            turn_square(normed[:, 2, :]).then_inc(normed_turned, 1)
            keep_warm(WARM_SHIFT)
            pe.wait_ge(xr_done, 1)
            for a in range(DH):
                last = nc.tensor.matmul(r_ps, xr_t[:, a, :], w[:, WB_FR + a, :], start=(a == 0), stop=(a == DH - 1))
            last.then_inc(r_projected, 1)
            pe.wait_ge(xk_done, 1)
            for b in range(DH):
                for a in range(DH):
                    last = nc.tensor.matmul(k_t_ps[b], w[:, WB_FK + a, b * P:(b + 1) * P], xk_t[:, a, :],
                                            start=(a == 0), stop=(a == DH - 1))
                last.then_inc(k_projected, 1)
            for a in range(DH):
                pe.wait_ge(k_act_done, a + 1)
                last = nc.tensor.matmul(mix_ps, k_act[:, a, :], w[:, WB_FV + a, :], start=(a == 0), stop=(a == DH - 1))
            last.then_inc(mix_done, 1)


def constants():
    c = np.zeros((P, C_ALL), np.float32)
    head = np.arange(P) // HEAD_D
    c[:, C_MASK:C_MASK + P] = (head[:, None] == head[None, :]) * np.float32(HEAD_D ** -0.5)
    power = np.arange(0, HEAD_D, 2).astype(np.float64)
    freqs = np.where(power < 10, 10000.0 ** -power, 0.0).astype(np.float32)
    angles = np.arange(L, dtype=np.float32)[:, None] * freqs[None, :]
    cos, sin = np.cos(angles), np.sin(angles)
    c[:, C_COS:C_COS + D] = np.tile(np.repeat(cos, 2, axis=1), (1, HEADS))
    c[:, C_SIN:C_SIN + D] = np.tile(np.stack([-sin, sin], axis=-1).reshape(L, HEAD_D), (1, HEADS))
    return c


def kernel(**inputs):
    import concourse.bacc as bacc
    from concourse.bass_utils import run_bass_kernel_spmd

    a = {name: np.asarray(value) for name, value in inputs.items()}

    def blocks(m):
        return [m[i:i + P] for i in range(0, m.shape[0], P)]

    packed = blocks(a["L0_xattn_W_qv"]) + blocks(a["L0_attn_Wq"]) + blocks(a["L0_attn_Wk"]) \
        + blocks(a["L0_attn_Wv"]) + blocks(a["L0_attn_Wo"]) + blocks(a["L0_ffn_W_k"].T) + blocks(a["L0_ffn_W_r"].T) + blocks(a["L0_ffn_W_v"].T)
    columns = [a["L0_xattn_w_sim"].reshape(3 * DH, P), a["L0_ffn_mu_r"].reshape(DH, P), a["L0_ffn_mu_k"].reshape(DH, P)]
    rows = [a["L0_xattn_b_qv"], a["L0_attn_bo"], a["L0_attn_bq"], a["L0_attn_bk"], a["L0_attn_bv"], a["L0_xattn_b_sim"]]
    arrays = {
        "x": a["x"].reshape(L, D),
        "ctx": a["ctx_1024"].reshape(S, D),
        "weights": np.concatenate(packed, axis=1),
        "vec": np.concatenate(columns, axis=0).T,
        "bias": np.concatenate(rows).reshape(1, BR),
        "const": constants(),
    }
    arrays = {name + "_dram": np.ascontiguousarray(value) for name, value in arrays.items()}

    nc = bacc.Bacc("TRN2", target_bir_lowering=False, num_devices=1)
    args = [nc.dram_tensor(name, value.shape, F32, kind="ExternalInput").ap() for name, value in arrays.items()]
    out = nc.dram_tensor("out_dram", (L, D), F32, kind="ExternalOutput").ap()
    build(nc, *args, out)
    result = run_bass_kernel_spmd(nc, [arrays], core_ids=[0])
    return result.results[0]["out_dram"].reshape(1, L, D)
```

```python
from contextlib import ExitStack

import numpy as np

import concourse.bass as bass
from concourse import mybir

P = 128
F32 = mybir.dt.float32
F32R = mybir.dt.float32r
BF16 = mybir.dt.bfloat16
ALU = mybir.AluOpType
ACT = mybir.ActivationFunctionType
AX_X = mybir.AxisListType.X

L = 128
D = 256
DH = D // P
HEADS = 16
HEAD_D = D // HEADS
S = 12544
TILES = 4
CHUNK = TILES * P
RING = 4
FULL = S // CHUNK
LAST_TILES = (S - FULL * CHUNK) // P
CHUNKS = FULL + 1
HW1_SLOT = CHUNKS - 3
LOOPED = (FULL - RING) // RING * RING
EPS = 1e-5
WARM_START, WARM_NORM_1, WARM_COPY, WARM_NORM_2, WARM_SHIFT = 9, 2, 2, 8, 4
WARM_Q, WARM_HEADS = 2, 2
FAR_BELOW = 3.0e38

WB_QV = 0
WB_Q = 4 * DH
WB_K = WB_Q + DH
WB_V = WB_K + DH
WB_O = WB_V + DH
WB_FK = WB_O + DH
WB_FR = WB_FK + DH
WB_FV = WB_FR + DH
WB = WB_FV + DH

VC_W1, VC_W2, VC_W3, VC_MUR, VC_MUK = (DH * n for n in range(5))
BR_QV, BR_O, BR_Q, BR_K, BR_V, BR_SIM = (D * n for n in range(6))
BR = 5 * D + 1
C_MASK, C_COS, C_SIN, C_ALL = 0, P, P + D, P + 2 * D


def build(nc, x, ctx_in, weights_in, vec_in, bias_in, const_in, out):
    ctx_full = ctx_in[0:FULL * CHUNK, :].rearrange("(k p t) d -> k p (t d)", p=P, t=TILES)
    ctx_last = ctx_in[FULL * CHUNK:S, :].rearrange("(p t) d -> p (t d)", t=LAST_TILES)

    with ExitStack() as stack:
        def sb(name, shape, dt=F32):
            return stack.enter_context(nc.sbuf_tensor(name, shape, dt))

        def ps(name, shape, dt=F32):
            return stack.enter_context(nc.psum_tensor(name, shape, dt))

        def sem(name):
            return stack.enter_context(nc.semaphore(name))

        const = sb("const", [P, C_ALL])
        block_mask = const[:, C_MASK:C_MASK + P]
        rope_cos = const[:, C_COS:C_COS + D]
        rope_sin = const[:, C_SIN:C_SIN + D]
        ident = sb("ident", [P, P])
        ones = sb("ones", [P, P])
        idle = sb("idle", [P, CHUNK], BF16)
        w = sb("w", [P, WB, D])
        vec = sb("vec", [P, 5 * DH])
        bias = sb("bias", [1, BR])
        x_sb = sb("x_sb", [P, D])
        ctx_rows = sb("ctx_rows", [P, RING, TILES, D])

        ctx_high = sb("ctx_high", [P, 2, DH, CHUNK], F32R)
        ctx_low = sb("ctx_low", [P, 2, DH, CHUNK], F32R)
        probs = sb("probs", [P, 2, CHUNK])
        rows_high = sb("rows_high", [P, RING, TILES, D], F32R)
        rows_low = sb("rows_low", [P, RING, TILES, D], F32R)
        turned_high = sb("turned_high", [P, 2, TILES, P], F32R)
        turned_low = sb("turned_low", [P, 2, TILES, P], F32R)
        unused = sb("unused", [P, CHUNK], BF16)
        neg_max = sb("neg_max", [P, RING])
        rescale = sb("rescale", [P, RING])
        row_sum = sb("row_sum", [P, RING])
        acc = sb("acc", [P, D])
        total = sb("total", [P, 1])

        ln_six = sb("ln_six", [P, 3, 6])
        ln_mv = sb("ln_mv", [P, 3, 2])
        ln_var = sb("ln_var", [P, 3])
        ln_rstd = sb("ln_rstd", [P, 3])
        minus_half = sb("minus_half", [P, 1])
        normed = sb("normed", [P, 3, D])
        normed_t = sb("normed_t", [P, 2, DH, P])
        q_t = sb("q_t", [P, DH, P])
        q_high = sb("q_high", [P, DH, P], F32R)
        q_low = sb("q_low", [P, DH, P], F32R)
        warm = sb("warm", [P, 1])
        sigmoid_warm = sb("sigmoid_warm", [P, 1])

        hw1 = sb("hw1", [P, 1])
        sim_max = sb("sim_max", [P, 1])
        batt_neg_max = sb("batt_neg_max", [P, 1])
        batt = sb("batt", [P, 1])
        batt_inv = sb("batt_inv", [P, 1])
        hc_bar = sb("hc_bar", [P, DH])
        hc_hat_t = sb("hc_hat_t", [P, DH, P])
        total_inv = sb("total_inv", [P, 1])
        acc_factor = sb("acc_factor", [P, 1])
        acc_scaled = sb("acc_scaled", [P, D])
        hq = sb("hq", [P, D])
        hq_t = sb("hq_t", [P, DH, P])
        h_hq_t = sb("h_hq_t", [P, DH, P])
        x1 = sb("x1", [P, D])

        with_cos = sb("with_cos", [P, 2, D])
        with_sin = sb("with_sin", [P, 2, D])
        rotated = sb("rotated", [P, 2, D])
        v = sb("v", [P, D])
        q_rot_t = sb("q_rot_t", [P, DH, P])
        kv = sb("kv", [P, DH, P])
        heads_t = sb("heads_t", [P, DH, P])
        x2 = sb("x2", [P, D])

        shifted = sb("shifted", [P, DH, P + 1])
        step_t = sb("step_t", [P, DH, P])
        xk_t = sb("xk_t", [P, DH, P])
        xr_t = sb("xr_t", [P, DH, P])
        k_relu = sb("k_relu", [P, DH, P])
        k_act = sb("k_act", [P, DH, P])
        gate = sb("gate", [P, D])
        mixed_out = sb("mixed_out", [P, D])
        x3 = sb("x3", [P, D])

        ctx_turned_ps = ps("ctx_turned_ps", [P, DH, CHUNK])
        scores_ps = ps("scores_ps", [P, 2, CHUNK])
        probs_turned_ps = ps("probs_turned_ps", [P, 2, CHUNK])
        mixed_ps = ps("mixed_ps", [P, CHUNK])
        side_ps = ps("side_ps", [P, CHUNK])
        turned_halves = (ctx_turned_ps[:, 0, :], ctx_turned_ps[:, 1, :])
        second_turned = (probs_turned_ps[:, 0, :], mixed_ps[:, :])
        hcq_ps = side_ps[:, 0:D]
        turn_ps = probs_turned_ps[:, 0, 0:D].rearrange("p (a l) -> p a l", a=DH)
        idle_ps = probs_turned_ps[:, 1, :]
        q_ps = scores_ps[:, 0, 0:D]
        k_ps = ctx_turned_ps[:, 0, 0:D]
        v_ps = mixed_ps[:, 0:D]
        kv_ps = ctx_turned_ps[:, 1, 0:D].rearrange("p (a l) -> p a l", a=DH)
        heads_ps = side_ps[:, 0:D].rearrange("p (a l) -> p a l", a=DH)
        x2_ps = scores_ps[:, 1, 0:D]
        r_ps = ctx_turned_ps[:, 0, 0:D]
        k_t_ps = (scores_ps[:, 0, 0:P], ctx_turned_ps[:, 1, 0:P])
        mix_ps = (mixed_ps[:, 0:P], side_ps[:, 0:P])

        x_loaded = sem("x_loaded")
        const_loaded = sem("const_loaded")
        vec_loaded = sem("vec_loaded")
        bias_loaded = sem("bias_loaded")
        w_qv_loaded = sem("w_qv_loaded")
        w_loaded = sem("w_loaded")
        ident_zeroed = sem("ident_zeroed")
        ident_done = sem("ident_done")
        idle_zeroed = sem("idle_zeroed")
        ones_set = sem("ones_set")
        ctx_loaded = [sem(f"ctx_loaded{r}") for r in range(RING)]
        out_stored = sem("out_stored")

        minus_half_set = sem("minus_half_set")
        shift_zeroed = sem("shift_zeroed")
        shifted_done = sem("shifted_done")
        stats_done = sem("stats_done")
        mv_done = sem("mv_done")
        var_done = sem("var_done")
        rstd_done = sem("rstd_done")
        normed_done = sem("normed_done")
        normed_turned = sem("normed_turned")
        normed_t_done = sem("normed_t_done")
        q_done = sem("q_done")
        q_high_done = sem("q_high_done")
        q_low_done = sem("q_low_done")

        ctx_turned = [sem(f"ctx_turned{a}") for a in range(DH)]
        high_done = sem("high_done")
        low_done = sem("low_done")
        scores_done = sem("scores_done")
        max_done = sem("max_done")
        exp_done = sem("exp_done")
        rescale_done = sem("rescale_done")
        probs_turned_done = sem("probs_turned_done")
        probs_high_done = sem("probs_high_done")
        probs_low_done = sem("probs_low_done")
        rows_high_done = sem("rows_high_done")
        rows_low_done = sem("rows_low_done")
        mixed_done = sem("mixed_done")
        acc_done = sem("acc_done")
        total_done = sem("total_done")

        hw1_done = sem("hw1_done")
        factor_done = sem("factor_done")
        acc_scaled_done = sem("acc_scaled_done")
        sim_max_done = sem("sim_max_done")
        sim_max_spread = sem("sim_max_spread")
        batt_max_done = sem("batt_max_done")
        batt_done = sem("batt_done")
        hc_bar_done = sem("hc_bar_done")
        batt_inv_done = sem("batt_inv_done")
        hc_bar_scaled = sem("hc_bar_scaled")
        hc_hat_done = sem("hc_hat_done")
        total_inv_done = sem("total_inv_done")
        hq_done = sem("hq_done")
        hq_turned = sem("hq_turned")
        hq_t_done = sem("hq_t_done")
        h_hq_done = sem("h_hq_done")
        hcq_done = sem("hcq_done")
        x1_done = sem("x1_done")

        q_projected = sem("q_projected")
        k_rows_projected = sem("k_rows_projected")
        v_projected = sem("v_projected")
        cos_done = sem("cos_done")
        sin_done = sem("sin_done")
        rotated_done = sem("rotated_done")
        v_done = sem("v_done")
        q_rot_turned = sem("q_rot_turned")
        q_rot_t_done = sem("q_rot_t_done")
        kv_done = sem("kv_done")
        kv_masked = sem("kv_masked")
        heads_done = sem("heads_done")
        heads_copied = sem("heads_copied")
        attn_done = sem("attn_done")
        x2_done = sem("x2_done")

        step_done = sem("step_done")
        xk_done = sem("xk_done")
        xr_done = sem("xr_done")
        k_projected = sem("k_projected")
        r_projected = sem("r_projected")
        k_relu_done = sem("k_relu_done")
        k_act_done = sem("k_act_done")
        gate_done = sem("gate_done")
        mix_done = sem("mix_done")
        mixed_out_done = sem("mixed_out_done")
        x3_done = sem("x3_done")

        block = stack.enter_context(nc.Block())

        def tiles_of(k):
            return LAST_TILES if isinstance(k, int) and k == CHUNKS - 1 else TILES

        @block.sync
        def _(sp):
            sp.dma_start(x_sb[:, :], x).then_inc(x_loaded, 16)
            for k in range(RING):
                sp.dma_start(ctx_rows[:, k, :, :], ctx_full[k].rearrange("p (t d) -> p t d", t=TILES))\
                    .then_inc(ctx_loaded[k], 16)
            with sp.Fori(0, (FULL - RING) // RING) as turn_of_ring:
                base = turn_of_ring * RING
                for u in range(RING):
                    sp.wait_ge(ctx_turned[DH - 1], base + (u + 1))
                    sp.wait_ge(rows_low_done, base + (u + 1))
                    src = ctx_full[bass.ds(base + (u + RING), 1), :, :]
                    sp.dma_start(ctx_rows[:, u, :, :], src.rearrange("k p (t d) -> p (k t) d", t=TILES))\
                        .then_inc(ctx_loaded[u], 16)
            k = CHUNKS - 1
            sp.wait_ge(ctx_turned[DH - 1], k - RING + 1)
            sp.wait_ge(rows_low_done, k - RING + 1)
            sp.dma_start(ctx_rows[:, k % RING, 0:LAST_TILES, :],
                         ctx_last.rearrange("p (t d) -> p t d", t=LAST_TILES)).then_inc(ctx_loaded[k % RING], 16)
            blocks_in = weights_in.rearrange("p (b n) -> p b n", b=WB)
            sp.dma_start(w[:, 0:WB_Q, :], blocks_in[:, 0:WB_Q, :]).then_inc(w_qv_loaded, 16)
            sp.dma_start(w[:, WB_Q:WB, :], blocks_in[:, WB_Q:WB, :]).then_inc(w_loaded, 16)
            sp.dma_start(const[:, :], const_in).then_inc(const_loaded, 16)
            sp.wait_ge(x3_done, DH)
            sp.dma_start(out, x3[:, :]).then_inc(out_stored, 16)
            sp.wait_ge(out_stored, 16)

        @block.gpsimd
        def _(pool):
            nc.gpsimd.memset(minus_half[:, :], -0.5).then_inc(minus_half_set, 1)
            nc.gpsimd.memset(ident[:, :], 0.0).then_inc(ident_zeroed, 1)
            pool.wait_ge(ident_zeroed, 1)
            nc.gpsimd.affine_select(out=ident[:, :], in_=ident[:, :], compare_op=ALU.not_equal, fill=1.0, base=0,
                                    pattern=[[-1, P]], channel_multiplier=1).then_inc(ident_done, 1)
            nc.gpsimd.memset(shifted[:, :, 0:1], 0.0).then_inc(shift_zeroed, 1)
            pool.wait_ge(minus_half_set, 1)

            def power(n):
                pool.wait_ge(var_done, n + 1)
                nc.gpsimd.tensor_tensor(out=ln_rstd[:, n:n + 1], in0=ln_var[:, n:n + 1], in1=minus_half[:, :],
                                        op=ALU.pow).then_inc(rstd_done, 1)

            def take_rows_low(k, u):
                tiles = tiles_of(k)
                pool.wait_ge(rows_high_done, k + 1)
                nc.gpsimd.tensor_tensor(out=rows_low[:, u, 0:tiles, :], in0=ctx_rows[:, u, 0:tiles, :],
                                        in1=rows_high[:, u, 0:tiles, :].bitcast(F32), op=ALU.subtract)\
                    .then_inc(rows_low_done, 1)

            power(0)
            for k in range(2):
                take_rows_low(k, k)
            with pool.Fori(0, LOOPED // RING) as turn_of_ring:
                base = turn_of_ring * RING
                for u in range(RING):
                    take_rows_low(base + (u + 2), (u + 2) % RING)
            for k in range(LOOPED + 2, CHUNKS):
                take_rows_low(k, k % RING)
            power(1)
            power(2)

        @block.scalar
        def _(act):
            act.wait_ge(minus_half_set, 1)
            nc.scalar.activation(warm[:, :], minus_half[:, :], ACT.Exp)
            act.dma_start(vec[:, :], vec_in).then_inc(vec_loaded, 16)
            act.dma_start(bias[:, :], bias_in).then_inc(bias_loaded, 16)

            def take_high(k, u, turned=turned_halves):
                width = tiles_of(k) * P
                for a in range(DH):
                    act.wait_ge(ctx_turned[a], k + 1)
                    nc.scalar.activation(ctx_high[:, u % 2, a, 0:width], turned[a][:, 0:width],
                                         ACT.Copy).then_inc(high_done, 1)

            def exps(k, u):
                width = tiles_of(k) * P
                act.wait_ge(max_done, k + 2)
                nc.scalar.activation(probs[:, u % 2, 0:width], scores_ps[:, u % 2, 0:width], ACT.Exp,
                                     bias=neg_max[:, u:u + 1], accum_out=row_sum[:, u:u + 1])\
                    .then_inc(exp_done, 1)
                before = (u - 1) % RING
                nc.scalar.activation(rescale[:, u:u + 1], neg_max[:, before:before + 1], ACT.Exp,
                                     bias=neg_max[:, u:u + 1], scale=-1.0).then_inc(rescale_done, 1)

            def probs_high(k, u):
                for half in range(tiles_of(k) // 2):
                    act.wait_ge(probs_turned_done, 2 * k + (half + 1))
                    nc.scalar.activation(turned_high[:, u % 2, 2 * half:2 * half + 2, :],
                                         probs_turned_ps[:, half, 0:2 * P].rearrange("p (t l) -> p t l", t=2),
                                         ACT.Copy).then_inc(probs_high_done, 1)

            def take_rows_high(k, u):
                tiles = tiles_of(k)
                nc.scalar.activation(rows_high[:, u, 0:tiles, :], ctx_rows[:, u, 0:tiles, :], ACT.Copy)\
                    .then_inc(rows_high_done, 1)

            act.wait_ge(ctx_loaded[0], 16)
            take_rows_high(0, 0)
            act.wait_ge(q_done, 1)
            nc.scalar.activation(q_high[:, :, :], q_t[:, :, :], ACT.Copy).then_inc(q_high_done, 1)
            take_high(0, 0)
            take_high(1, 1, second_turned)
            act.wait_ge(q_done, 1)
            nc.scalar.activation(normed_t[:, 0, :, :], side_ps[:, 0:D].rearrange("p (a l) -> p a l", a=DH),
                                 ACT.Copy).then_inc(normed_t_done, 1)
            act.wait_ge(ctx_loaded[1], 16)
            take_rows_high(1, 1)
            exps(0, 0)
            with act.Fori(0, LOOPED // RING) as turn_of_ring:
                base = turn_of_ring * RING
                for u in range(RING):
                    probs_high(base + u, u)
                    take_high(base + (u + 2), (u + 2) % RING)
                    exps(base + (u + 1), (u + 1) % RING)
                    if u + 2 < RING:
                        act.wait_ge(ctx_loaded[u + 2], turn_of_ring * 16 + 16)
                    else:
                        act.wait_ge(ctx_loaded[u + 2 - RING], turn_of_ring * 16 + 32)
                    take_rows_high(base + (u + 2), (u + 2) % RING)
            for k in range(LOOPED, CHUNKS):
                probs_high(k, k % RING)
                if k + 2 < CHUNKS:
                    take_high(k + 2, (k + 2) % RING)
                if k + 1 < CHUNKS:
                    exps(k + 1, (k + 1) % RING)
                if k + 2 < CHUNKS:
                    act.wait_ge(ctx_loaded[(k + 2) % RING], 16 * ((k + 2) // RING + 1))
                    take_rows_high(k + 2, (k + 2) % RING)

            act.wait_ge(batt_max_done, 1)
            nc.scalar.activation(batt[:, :], sim_max[:, :], ACT.Exp, bias=batt_neg_max[:, :]).then_inc(batt_done, 1)
            nc.scalar.activation(sigmoid_warm[:, :], minus_half[:, :], ACT.Sigmoid)
            act.wait_ge(hc_bar_scaled, 1)
            for a in range(DH):
                nc.scalar.activation(hc_hat_t[:, a, :], normed_t[:, 0, a, :], ACT.Identity, scale=hc_bar[:, a:a + 1])\
                    .then_inc(hc_hat_done, 1)
            act.wait_ge(hq_turned, 1)
            nc.scalar.activation(hq_t[:, :, :], turn_ps, ACT.Copy).then_inc(hq_t_done, 1)

            act.wait_ge(normed_done, 2)
            nc.scalar.activation(x1[:, :], hcq_ps, ACT.Copy).then_inc(x1_done, 1)
            act.wait_ge(normed_turned, 2)
            nc.scalar.activation(normed_t[:, 1, :, :], turn_ps, ACT.Copy).then_inc(normed_t_done, 1)
            act.wait_ge(v_projected, 1)
            nc.scalar.activation(v[:, :], v_ps, ACT.Copy).then_inc(v_done, 1)
            act.wait_ge(q_rot_turned, 1)
            nc.scalar.activation(q_rot_t[:, :, :], turn_ps, ACT.Copy).then_inc(q_rot_t_done, 1)
            act.wait_ge(heads_done, 1)
            nc.scalar.activation(heads_t[:, :, :], heads_ps, ACT.Copy).then_inc(heads_copied, 1)

            act.wait_ge(normed_done, 3)
            nc.scalar.activation(x2[:, :], x2_ps, ACT.Copy).then_inc(x2_done, 1)
            act.wait_ge(shift_zeroed, 1)
            act.wait_ge(normed_turned, 3)
            for a in range(DH):
                nc.scalar.activation(shifted[:, a, 1:P + 1], turn_ps[:, a, :], ACT.Copy).then_inc(shifted_done, 1)
            for b in range(DH):
                act.wait_ge(k_projected, b + 1)
                nc.scalar.activation(k_relu[:, b, :], k_t_ps[b], ACT.Relu).then_inc(k_relu_done, 1)
            act.wait_ge(r_projected, 1)
            nc.scalar.activation(gate[:, :], r_ps, ACT.Sigmoid).then_inc(gate_done, 1)

        @block.vector
        def _(dve):
            def layer_norm(n, source):
                nc.vector.bn_stats(ln_six[:, n, :], source).then_inc(stats_done, 1)
                dve.wait_ge(stats_done, n + 1)
                nc.vector.bn_aggr(ln_mv[:, n, :], ln_six[:, n, :]).then_inc(mv_done, 1)
                dve.wait_ge(mv_done, n + 1)
                nc.vector.tensor_scalar_add(ln_var[:, n:n + 1], ln_mv[:, n, 1:2], EPS).then_inc(var_done, 1)
                dve.wait_ge(rstd_done, n + 1)
                nc.vector.tensor_scalar(normed[:, n, :], source, ln_mv[:, n, 0:1], ln_rstd[:, n:n + 1],
                                        ALU.subtract, ALU.mult).then_inc(normed_done, 1)

            def take_low(k, u, turned=turned_halves, halves=range(DH)):
                width = tiles_of(k) * P
                for a in halves:
                    dve.wait_ge(high_done, k * DH + (a + 1))
                    nc.vector.tensor_tensor(out=ctx_low[:, u % 2, a, 0:width], in0=turned[a][:, 0:width],
                                            in1=ctx_high[:, u % 2, a, 0:width].bitcast(F32), op=ALU.subtract)\
                        .then_inc(low_done, 1)

            def running_max(k, u):
                width = tiles_of(k) * P
                before = (u - 1) % RING
                dve.wait_ge(scores_done, k + 1)
                dve.wait_ge(max_done, k + 1)
                nc.vector.tensor_scalar(unused[:, 0:width], scores_ps[:, u % 2, 0:width], -1.0,
                                        neg_max[:, before:before + 1], ALU.mult, ALU.min,
                                        accum_out=neg_max[:, u:u + 1]).then_inc(max_done, 1)

            def probs_low(k, u):
                for half in range(tiles_of(k) // 2):
                    dve.wait_ge(probs_high_done, 2 * k + (half + 1))
                    nc.vector.tensor_tensor(out=turned_low[:, u % 2, 2 * half:2 * half + 2, :],
                                            in0=probs_turned_ps[:, half, 0:2 * P].rearrange("p (t l) -> p t l", t=2),
                                            in1=turned_high[:, u % 2, 2 * half:2 * half + 2, :].bitcast(F32),
                                            op=ALU.subtract).then_inc(probs_low_done, 1)

            def add_total(k, u):
                dve.wait_ge(exp_done, k + 1)
                dve.wait_ge(rescale_done, k + 1)
                dve.wait_ge(total_done, k + 1)
                nc.vector.scalar_tensor_tensor(total[:, :], total[:, :], rescale[:, u:u + 1], row_sum[:, u:u + 1],
                                               ALU.mult, ALU.add).then_inc(total_done, 1)

            def accumulate(k, u):
                add_total(k, u)
                dve.wait_ge(mixed_done, k + 1)
                if isinstance(k, int) and k == HW1_SLOT:
                    nc.vector.tensor_copy(hw1[:, :], mixed_ps[:, D:D + 1]).then_inc(hw1_done, 1)
                dve.wait_ge(acc_done, k + 1)
                nc.vector.scalar_tensor_tensor(acc[:, :], acc[:, :], rescale[:, u:u + 1], mixed_ps[:, 0:D],
                                               ALU.mult, ALU.add).then_inc(acc_done, 1)

            nc.vector.memset(idle[:, :], 0.0).then_inc(idle_zeroed, 1)
            nc.vector.memset(neg_max[:, RING - 1:RING], FAR_BELOW).then_inc(max_done, 1)
            nc.vector.memset(acc[:, :], 0.0).then_inc(acc_done, 1)
            nc.vector.memset(total[:, :], 0.0).then_inc(total_done, 1)
            nc.vector.memset(ones[:, :], 1.0).then_inc(ones_set, 1)
            dve.wait_ge(x_loaded, 16)
            layer_norm(0, x_sb[:, :])
            dve.wait_ge(vec_loaded, 16)
            dve.wait_ge(normed_turned, 1)
            for a in range(DH):
                last = nc.vector.tensor_scalar(q_t[:, a, :], side_ps[:, a * P:(a + 1) * P],
                                               vec[:, VC_W3 + a:VC_W3 + a + 1], vec[:, VC_W2 + a:VC_W2 + a + 1],
                                               ALU.mult, ALU.add)
            last.then_inc(q_done, 1)
            dve.wait_ge(q_high_done, 1)
            nc.vector.tensor_tensor(out=q_low[:, :, :], in0=q_t[:, :, :], in1=q_high[:, :, :].bitcast(F32),
                                    op=ALU.subtract).then_inc(q_low_done, 1)
            take_low(0, 0)
            take_low(1, 1, second_turned, halves=[0])
            running_max(0, 0)
            take_low(1, 1, second_turned, halves=[1])
            with dve.Fori(0, LOOPED // RING) as turn_of_ring:
                base = turn_of_ring * RING
                for u in range(RING):
                    probs_low(base + u, u)
                    running_max(base + (u + 1), (u + 1) % RING)
                    take_low(base + (u + 2), (u + 2) % RING)
                    accumulate(base + u, u)
            for k in range(LOOPED, CHUNKS - 1):
                probs_low(k, k % RING)
                running_max(k + 1, (k + 1) % RING)
                if k + 2 < CHUNKS:
                    take_low(k + 2, (k + 2) % RING)
                else:
                    u = (k + 1) % RING
                    dve.wait_ge(hw1_done, 1)
                    dve.wait_ge(max_done, CHUNKS + 1)
                    nc.vector.tensor_tensor(out=sim_max[:, :], in0=hw1[:, :], in1=neg_max[:, u:u + 1],
                                            op=ALU.subtract).then_inc(sim_max_done, 1)
                accumulate(k, k % RING)
            k, u = CHUNKS - 1, (CHUNKS - 1) % RING
            dve.wait_ge(sim_max_spread, 1)
            nc.vector.tensor_reduce(batt_neg_max[:, :], scores_ps[:, 1, 0:P], axis=AX_X, op=ALU.max,
                                    negate=True).then_inc(batt_max_done, 1)
            probs_low(k, u)
            add_total(k, u)
            dve.wait_ge(total_done, CHUNKS + 1)
            nc.vector.reciprocal(total_inv[:, :], total[:, :]).then_inc(total_inv_done, 1)
            dve.wait_ge(hc_bar_done, 1)
            nc.vector.reciprocal(batt_inv[:, :], scores_ps[:, 0, DH:DH + 1]).then_inc(batt_inv_done, 1)
            dve.wait_ge(batt_inv_done, 1)
            nc.vector.tensor_scalar(hc_bar[:, :], scores_ps[:, 0, 0:DH], batt_inv[:, :], None, ALU.mult)\
                .then_inc(hc_bar_scaled, 1)
            dve.wait_ge(total_inv_done, 1)
            nc.vector.tensor_tensor(out=acc_factor[:, :], in0=total_inv[:, :], in1=rescale[:, u:u + 1],
                                    op=ALU.mult).then_inc(factor_done, 1)
            dve.wait_ge(factor_done, 1)
            dve.wait_ge(acc_done, CHUNKS)
            nc.vector.tensor_scalar(acc_scaled[:, :], acc[:, :], acc_factor[:, :], None, ALU.mult)\
                .then_inc(acc_scaled_done, 1)
            dve.wait_ge(acc_scaled_done, 1)
            dve.wait_ge(mixed_done, CHUNKS)
            nc.vector.scalar_tensor_tensor(hq[:, :], mixed_ps[:, 0:D], total_inv[:, :], acc_scaled[:, :],
                                           ALU.mult, ALU.add).then_inc(hq_done, 1)
            dve.wait_ge(hq_t_done, 1)
            nc.vector.tensor_tensor(out=h_hq_t[:, :, :], in0=normed_t[:, 0, :, :], in1=hq_t[:, :, :],
                                    op=ALU.mult).then_inc(h_hq_done, 1)

            dve.wait_ge(hcq_done, 1)
            layer_norm(1, hcq_ps)
            dve.wait_ge(const_loaded, 16)
            for done, (n, part_ps, projected) in enumerate(((1, k_ps, k_rows_projected), (0, q_ps, q_projected))):
                dve.wait_ge(projected, 1)
                nc.vector.tensor_tensor(out=with_cos[:, n, :], in0=part_ps, in1=rope_cos, op=ALU.mult)\
                    .then_inc(cos_done, 1)
                nc.vector.tensor_tensor(out=with_sin[:, n, :].rearrange("p (m c) -> p m c", c=2),
                                        in0=part_ps.rearrange("p (m c) -> p m c", c=2)[:, :, ::-1],
                                        in1=rope_sin.rearrange("p (m c) -> p m c", c=2), op=ALU.mult)\
                    .then_inc(sin_done, 1)
                dve.wait_ge(cos_done, done + 1)
                dve.wait_ge(sin_done, done + 1)
                nc.vector.tensor_tensor(out=rotated[:, n, :], in0=with_cos[:, n, :], in1=with_sin[:, n, :],
                                        op=ALU.add).then_inc(rotated_done, 1)
            dve.wait_ge(kv_done, 1)
            nc.vector.tensor_tensor(out=kv[:, :, :], in0=kv_ps, in1=block_mask.unsqueeze(1).to_broadcast([P, DH, P]),
                                    op=ALU.mult).then_inc(kv_masked, 1)

            dve.wait_ge(attn_done, 1)
            layer_norm(2, x2_ps)
            for a in range(DH):
                dve.wait_ge(shifted_done, a + 1)
                nc.vector.tensor_tensor(out=step_t[:, a, :], in0=shifted[:, a, 1:P + 1], in1=shifted[:, a, 0:P],
                                        op=ALU.subtract).then_inc(step_done, 1)
            for mixed_t, col, done in ((xk_t, VC_MUK, xk_done), (xr_t, VC_MUR, xr_done)):
                for a in range(DH):
                    dve.wait_ge(step_done, a + 1)
                    nc.vector.scalar_tensor_tensor(mixed_t[:, a, :], step_t[:, a, :], vec[:, col + a:col + a + 1],
                                                   shifted[:, a, 0:P], ALU.mult, ALU.add).then_inc(done, 1)
            for b in range(DH):
                dve.wait_ge(k_relu_done, b + 1)
                nc.vector.tensor_tensor(out=k_act[:, b, :], in0=k_relu[:, b, :], in1=k_relu[:, b, :], op=ALU.mult)\
                    .then_inc(k_act_done, 1)
            dve.wait_ge(gate_done, 1)
            for c in range(DH):
                dve.wait_ge(mix_done, c + 1)
                nc.vector.tensor_tensor(out=mixed_out[:, c * P:(c + 1) * P], in0=mix_ps[c],
                                        in1=gate[:, c * P:(c + 1) * P], op=ALU.mult).then_inc(mixed_out_done, 1)
            dve.wait_ge(x2_done, 1)
            for c in range(DH):
                dve.wait_ge(mixed_out_done, c + 1)
                nc.vector.tensor_tensor(out=x3[:, c * P:(c + 1) * P], in0=mixed_out[:, c * P:(c + 1) * P],
                                        in1=x2[:, c * P:(c + 1) * P], op=ALU.add).then_inc(x3_done, 1)

        @block.tensor
        def _(pe):
            def keep_warm(n):
                for _ in range(n):
                    nc.tensor.matmul(idle_ps, idle[:, 0:P], idle[:, :], start=True, stop=True)

            def turn_square(source):
                for a in range(DH):
                    last = nc.tensor.transpose(turn_ps[:, a, :], source[:, a * P:(a + 1) * P], ident[:, :])
                return last

            def add_bias(out_ps, col, start=True):
                nc.tensor.matmul(out_ps, ones[0:1, :], bias[0:1, col:col + D], start=start, stop=False)

            def turn(k, u, turned=turned_halves):
                for a in range(DH):
                    for t in range(tiles_of(k)):
                        last = nc.tensor.transpose(turned[a][:, t * P:(t + 1) * P],
                                                   ctx_rows[:, u, t, a * P:(a + 1) * P], ident[:, :])
                    last.then_inc(ctx_turned[a], 1)

            def score_part(k, u, a, q_part, c_part, first=False, end=False):
                width = tiles_of(k) * P
                return nc.tensor.matmul(scores_ps[:, u % 2, 0:width], q_part[:, a, :], c_part[:, u % 2, a, 0:width],
                                        start=first, stop=end)

            def score_upper(k, u):
                for a in range(DH):
                    pe.wait_ge(high_done, k * DH + (a + 1))
                    score_part(k, u, a, q_high, ctx_high, first=(a == 0))
                if isinstance(k, int) and k == 0:
                    pe.wait_ge(q_low_done, 1)
                for a in range(DH):
                    score_part(k, u, a, q_low, ctx_high)

            def score_rest(k, u):
                for a in range(DH):
                    pe.wait_ge(low_done, k * DH + (a + 1))
                    last = score_part(k, u, a, q_high, ctx_low, end=(a == DH - 1))
                last.then_inc(scores_done, 1)

            def turn_probs(k, u):
                pe.wait_ge(exp_done, k + 1)
                for half in range(tiles_of(k) // 2):
                    for t in range(2):
                        col = (2 * half + t) * P
                        last = nc.tensor.transpose(probs_turned_ps[:, half, t * P:(t + 1) * P],
                                                   probs[:, u % 2, col:col + P], ident[:, :])
                    last.then_inc(probs_turned_done, 1)

            def mix(k, u):
                pe.wait_ge(acc_done, k + 1)
                if isinstance(k, int) and k == HW1_SLOT:
                    for a in range(DH):
                        nc.tensor.matmul(mixed_ps[:, D:D + 1], normed_t[:, 0, a, :], vec[:, VC_W1 + a:VC_W1 + a + 1],
                                         start=(a == 0), stop=False)
                    nc.tensor.matmul(mixed_ps[:, D:D + 1], ones[0:1, :], bias[0:1, BR_SIM:BR_SIM + 1],
                                     start=False, stop=True)
                tiles = tiles_of(k)
                pe.wait_ge(rows_low_done, k + 1)
                for t in range(tiles):
                    if t % 2 == 0:
                        pe.wait_ge(probs_low_done, 2 * k + (t // 2 + 1))
                    for probs_part, rows_part in ((turned_high, rows_high), (turned_high, rows_low),
                                                  (turned_low, rows_high)):
                        last = nc.tensor.matmul(mixed_ps[:, 0:D], probs_part[:, u % 2, t, :], rows_part[:, u, t, :],
                                                start=(t == 0 and rows_part is rows_high and probs_part is turned_high),
                                                stop=(t == tiles - 1 and probs_part is turned_low))
                last.then_inc(mixed_done, 1)

            def features(kind, source, halves=range(DH), start=False, stop=False):
                for a in halves:
                    last = nc.tensor.matmul(hcq_ps, source[:, a, :], w[:, WB_QV + kind * DH + a, :],
                                            start=start and a == 0, stop=stop and a == DH - 1)
                return last

            pe.wait_ge(idle_zeroed, 1)
            keep_warm(WARM_START)
            pe.wait_ge(ident_done, 1)
            pe.wait_ge(normed_done, 1)
            for a in range(DH):
                last = nc.tensor.transpose(side_ps[:, a * P:(a + 1) * P], normed[:, 0, a * P:(a + 1) * P], ident[:, :])
            last.then_inc(normed_turned, 1)
            pe.wait_ge(ctx_loaded[0], 16)
            turn(0, 0)
            pe.wait_ge(ctx_loaded[1], 16)
            turn(1, 1, second_turned)
            pe.wait_ge(q_high_done, 1)
            score_upper(0, 0)
            score_rest(0, 0)
            with pe.Fori(0, LOOPED // RING) as turn_of_ring:
                base = turn_of_ring * RING
                for u in range(RING):
                    score_upper(base + (u + 1), (u + 1) % RING)
                    turn_probs(base + u, u)
                    score_rest(base + (u + 1), (u + 1) % RING)
                    if u + 2 < RING:
                        pe.wait_ge(ctx_loaded[u + 2], turn_of_ring * 16 + 16)
                    else:
                        pe.wait_ge(ctx_loaded[u + 2 - RING], turn_of_ring * 16 + 32)
                    turn(base + (u + 2), (u + 2) % RING)
                    mix(base + u, u)
            pe.wait_ge(ones_set, 1)
            pe.wait_ge(bias_loaded, 16)
            pe.wait_ge(normed_t_done, 1)
            for k in range(LOOPED, CHUNKS - 1):
                score_upper(k + 1, (k + 1) % RING)
                turn_probs(k, k % RING)
                score_rest(k + 1, (k + 1) % RING)
                if k + 2 < CHUNKS:
                    pe.wait_ge(ctx_loaded[(k + 2) % RING], 16 * ((k + 2) // RING + 1))
                    turn(k + 2, (k + 2) % RING)
                else:
                    pe.wait_ge(w_qv_loaded, 16)
                    features(0, normed_t[:, 0, :, :], start=True)
                mix(k, k % RING)
            pe.wait_ge(sim_max_done, 1)
            nc.tensor.matmul(scores_ps[:, 1, 0:P], sim_max[:, 0:1].to_broadcast([P, P]), ident[:, :],
                             start=True, stop=True).then_inc(sim_max_spread, 1)
            turn_probs(CHUNKS - 1, (CHUNKS - 1) % RING)
            add_bias(hcq_ps, BR_QV, start=False)
            nc.tensor.matmul(hcq_ps, ident[:, :], x_sb[:, :], start=False, stop=False)
            pe.wait_ge(batt_done, 1)
            for a in range(DH):
                nc.tensor.matmul(scores_ps[:, 0, a:a + 1], normed[:, 0, a * P:(a + 1) * P], batt[:, :],
                                 start=True, stop=True)
            nc.tensor.matmul(scores_ps[:, 0, DH:DH + 1], ones[:, :], batt[:, :], start=True, stop=True)\
                .then_inc(hc_bar_done, 1)
            mix(CHUNKS - 1, (CHUNKS - 1) % RING)
            pe.wait_ge(hc_hat_done, 1)
            features(3, hc_hat_t, halves=[0])
            pe.wait_ge(hq_done, 1)
            turn_square(hq).then_inc(hq_turned, 1)
            pe.wait_ge(hc_hat_done, 2)
            features(3, hc_hat_t, halves=[1])
            pe.wait_ge(hq_t_done, 1)
            features(1, hq_t)
            pe.wait_ge(h_hq_done, 1)
            features(2, h_hq_t, stop=True).then_inc(hcq_done, 1)

            for out_ps, col in ((q_ps, BR_Q), (k_ps, BR_K), (v_ps, BR_V), (x2_ps, BR_O)):
                add_bias(out_ps, col)
            pe.wait_ge(w_loaded, 16)
            keep_warm(WARM_NORM_1)
            pe.wait_ge(normed_done, 2)
            turn_square(normed[:, 1, :]).then_inc(normed_turned, 1)
            keep_warm(WARM_COPY)
            pe.wait_ge(normed_t_done, 2)
            for out_ps, block_row, done in ((k_ps, WB_K, k_rows_projected), (q_ps, WB_Q, q_projected),
                                            (v_ps, WB_V, v_projected)):
                for a in range(DH):
                    last = nc.tensor.matmul(out_ps, normed_t[:, 1, a, :], w[:, block_row + a, :],
                                            start=False, stop=(a == DH - 1))
                last.then_inc(done, 1)
            pe.wait_ge(x1_done, 1)
            nc.tensor.matmul(x2_ps, ident[:, :], x1[:, :], start=False, stop=False)
            pe.wait_ge(rotated_done, 1)
            pe.wait_ge(v_done, 1)
            for a in range(DH):
                last = nc.tensor.matmul(kv_ps[:, a, :], rotated[:, 1, a * P:(a + 1) * P], v[:, a * P:(a + 1) * P],
                                        start=True, stop=True)
            last.then_inc(kv_done, 1)
            pe.wait_ge(rotated_done, 2)
            turn_square(rotated[:, 0, :]).then_inc(q_rot_turned, 1)
            keep_warm(WARM_Q)
            pe.wait_ge(q_rot_t_done, 1)
            pe.wait_ge(kv_masked, 1)
            for a in range(DH):
                last = nc.tensor.matmul(heads_ps[:, a, :], kv[:, a, :], q_rot_t[:, a, :], start=True, stop=True)
            last.then_inc(heads_done, 1)
            keep_warm(WARM_HEADS)
            pe.wait_ge(heads_copied, 1)
            for a in range(DH):
                last = nc.tensor.matmul(x2_ps, heads_t[:, a, :], w[:, WB_O + a, :], start=False, stop=(a == DH - 1))
            last.then_inc(attn_done, 1)

            keep_warm(WARM_NORM_2)
            pe.wait_ge(normed_done, 3)
            turn_square(normed[:, 2, :]).then_inc(normed_turned, 1)
            keep_warm(WARM_SHIFT)
            for a in range(DH):
                pe.wait_ge(xk_done, a + 1)
                for b in range(DH):
                    last = nc.tensor.matmul(k_t_ps[b], w[:, WB_FK + a, b * P:(b + 1) * P], xk_t[:, a, :],
                                            start=(a == 0), stop=(a == DH - 1))
                    if a == DH - 1:
                        last.then_inc(k_projected, 1)
            for a in range(DH):
                pe.wait_ge(xr_done, a + 1)
                last = nc.tensor.matmul(r_ps, xr_t[:, a, :], w[:, WB_FR + a, :], start=(a == 0), stop=(a == DH - 1))
            last.then_inc(r_projected, 1)
            for a in range(DH):
                pe.wait_ge(k_act_done, a + 1)
                for c in range(DH):
                    last = nc.tensor.matmul(mix_ps[c], k_act[:, a, :], w[:, WB_FV + a, c * P:(c + 1) * P],
                                            start=(a == 0), stop=(a == DH - 1))
                    if a == DH - 1:
                        last.then_inc(mix_done, 1)


def constants():
    c = np.zeros((P, C_ALL), np.float32)
    head = np.arange(P) // HEAD_D
    c[:, C_MASK:C_MASK + P] = (head[:, None] == head[None, :]) * np.float32(HEAD_D ** -0.5)
    power = np.arange(0, HEAD_D, 2).astype(np.float64)
    freqs = np.where(power < 10, 10000.0 ** -power, 0.0).astype(np.float32)
    angles = np.arange(L, dtype=np.float32)[:, None] * freqs[None, :]
    cos, sin = np.cos(angles), np.sin(angles)
    c[:, C_COS:C_COS + D] = np.tile(np.repeat(cos, 2, axis=1), (1, HEADS))
    c[:, C_SIN:C_SIN + D] = np.tile(np.stack([-sin, sin], axis=-1).reshape(L, HEAD_D), (1, HEADS))
    return c


def kernel(**inputs):
    import concourse.bacc as bacc
    from concourse.bass_utils import run_bass_kernel_spmd

    a = {name: np.asarray(value) for name, value in inputs.items()}

    def blocks(m):
        return [m[i:i + P] for i in range(0, m.shape[0], P)]

    packed = blocks(a["L0_xattn_W_qv"]) + blocks(a["L0_attn_Wq"]) + blocks(a["L0_attn_Wk"]) \
        + blocks(a["L0_attn_Wv"]) + blocks(a["L0_attn_Wo"]) + blocks(a["L0_ffn_W_k"].T) + blocks(a["L0_ffn_W_r"].T) + blocks(a["L0_ffn_W_v"].T)
    columns = [a["L0_xattn_w_sim"].reshape(3 * DH, P), a["L0_ffn_mu_r"].reshape(DH, P), a["L0_ffn_mu_k"].reshape(DH, P)]
    rows = [a["L0_xattn_b_qv"], a["L0_attn_bo"], a["L0_attn_bq"], a["L0_attn_bk"], a["L0_attn_bv"], a["L0_xattn_b_sim"]]
    arrays = {
        "x": a["x"].reshape(L, D),
        "ctx": a["ctx_1024"].reshape(S, D),
        "weights": np.concatenate(packed, axis=1),
        "vec": np.concatenate(columns, axis=0).T,
        "bias": np.concatenate(rows).reshape(1, BR),
        "const": constants(),
    }
    arrays = {name + "_dram": np.ascontiguousarray(value) for name, value in arrays.items()}

    nc = bacc.Bacc("TRN2", target_bir_lowering=False, num_devices=1)
    args = [nc.dram_tensor(name, value.shape, F32, kind="ExternalInput").ap() for name, value in arrays.items()]
    out = nc.dram_tensor("out_dram", (L, D), F32, kind="ExternalOutput").ap()
    build(nc, *args, out)
    result = run_bass_kernel_spmd(nc, [arrays], core_ids=[0])
    return result.results[0]["out_dram"].reshape(1, L, D)
```
